# Optimizing a Trainium2 kernel written in Bass

```python
import numpy as np
import jax
import jax.numpy as jnp

def _softmax(x, axis=-1):
    return jax.nn.softmax(x, axis=axis)

def _gelu(x):
    return jax.nn.gelu(x, approximate=True)

def _silu(x):
    return jax.nn.silu(x)

def _sigmoid(x):
    return jax.nn.sigmoid(x)

def _layernorm(x, axis=-1, eps=1e-05):
    m = jnp.mean(x, axis=axis, keepdims=True)
    v = jnp.var(x, axis=axis, keepdims=True)
    return (x - m) / jnp.sqrt(v + eps)

def _scatter_add(tgt, idx, src, axis=0):
    return tgt.at[idx].add(src)

def _segment_sum(src, seg, n):
    return jax.ops.segment_sum(src, seg, n)
kernel_name = 'mk_xattn_ffn_d2_seqx_r8_4e3fd6'

def setup_inputs(seed: int=0):
    np.random.seed(seed)
    _w = jnp.asarray

    def _rec_inputs():
        import jax
        import jax.numpy as jnp
        _rk = jax.random.key(seed)
        x = -0.0002928 + 1 * jax.random.normal(jax.random.fold_in(_rk, 1), (4, 512, 128), jnp.float32)
        _lenS = 512 - jax.random.randint(jax.random.fold_in(_rk, 7), (4,), 0, max(1, 512 // 4) + 1, jnp.int32)
        _lenS2 = 77 - jax.random.randint(jax.random.fold_in(_rk, 8), (4,), 0, max(1, 77 // 4) + 1, jnp.int32)
        _ctx_1024P = jax.random.normal(jax.random.fold_in(_rk, 11), (4, 16, 128), jnp.float32)
        _ctx_1024c = jax.random.dirichlet(jax.random.fold_in(_rk, 511), 0.3 * jnp.ones((16,), jnp.float32), (4, 77))
        _ctx_1024t = jnp.einsum('bsk,bkd->bsd', _ctx_1024c, _ctx_1024P)
        _ctx_1024t = _ctx_1024t * jax.lax.rsqrt(jnp.mean(jnp.square(_ctx_1024t)) + 1e-12) * 0.953939
        ctx_1024 = -1.39393e-06 + 0.999914 * (_ctx_1024t + 0.3 * jax.random.normal(jax.random.fold_in(_rk, 611), (4, 77, 128), jnp.float32))
        return (x, ctx_1024)
    x, ctx_1024 = _rec_inputs()

    def _L0_xattn_setup():
        import jax, jax.numpy as jnp
        import numpy as np
        D_MODEL = 128
        NUM_HEADS = 16
        HEAD_DIM = D_MODEL // NUM_HEADS
        key = jax.random.key(seed)
        ks = jax.random.split(key, 10)
        B, SQ, SKV = (2, 256, 256)
        s = 1.0 / np.sqrt(D_MODEL)
        inp = {'query': jax.random.normal(ks[0], (B, SQ, D_MODEL), jnp.float32), 'key_value': jax.random.normal(ks[1], (B, SKV, D_MODEL), jnp.float32), 'Wq': jax.random.normal(ks[2], (D_MODEL, D_MODEL), jnp.float32) * s, 'bq': jnp.zeros((D_MODEL,), jnp.float32), 'Wk': jax.random.normal(ks[3], (D_MODEL, D_MODEL), jnp.float32) * s, 'bk': jnp.zeros((D_MODEL,), jnp.float32), 'Wv': jax.random.normal(ks[4], (D_MODEL, D_MODEL), jnp.float32) * s, 'bv': jnp.zeros((D_MODEL,), jnp.float32), 'Wo': jax.random.normal(ks[5], (D_MODEL, D_MODEL), jnp.float32) * s, 'bo': jnp.zeros((D_MODEL,), jnp.float32)}
        return inp
    _L0_xattn_all = _L0_xattn_setup()
    _L0_xattn_in = {k: v for k, v in _L0_xattn_all.items() if k in ('Wq', 'bq', 'Wk', 'bk', 'Wv', 'bv', 'Wo', 'bo')}
    del _L0_xattn_all

    def _L0_ffn_setup():
        import jax, jax.numpy as jnp
        import numpy as np
        EPS = 1e-05

        def _quantize(W):
            gamma = jnp.mean(jnp.abs(W))
            return jnp.clip(jnp.round(W / (gamma + EPS)), -1.0, 1.0)
        key = jax.random.key(seed)
        k_x, k_w1, k_b1, k_w2, k_b2 = jax.random.split(key, 5)
        n_embd = 128
        d_ff = 4 * n_embd
        B, S = (4, 512)
        bound1 = 1.0 / np.sqrt(n_embd)
        bound2 = 1.0 / np.sqrt(d_ff)
        x = jax.random.normal(k_x, (B, S, n_embd), dtype=jnp.float32)
        W1 = jax.random.uniform(k_w1, (d_ff, n_embd), jnp.float32, -bound1, bound1)
        b1 = jax.random.uniform(k_b1, (d_ff,), jnp.float32, -bound1, bound1)
        W2 = jax.random.uniform(k_w2, (n_embd, d_ff), jnp.float32, -bound2, bound2)
        b2 = jax.random.uniform(k_b2, (n_embd,), jnp.float32, -bound2, bound2)
        return {'x': x, 'W1': W1, 'b1': b1, 'W2': W2, 'b2': b2}
    _L0_ffn_all = _L0_ffn_setup()
    _L0_ffn_in = {k: v for k, v in _L0_ffn_all.items() if k in ('W1', 'b1', 'W2', 'b2')}
    del _L0_ffn_all

    def _L1_xattn_setup():
        import jax, jax.numpy as jnp
        import numpy as np
        EMBED = 128
        B, I, J = (8, 256, 256)
        SCALE = EMBED ** (-0.5)
        key = jax.random.key(seed)
        ks = jax.random.split(key, 5)
        s = EMBED ** (-0.5)
        return {'q_in': jax.random.normal(ks[0], (B, I, EMBED), dtype=jnp.float32), 'k_v': jax.random.normal(ks[1], (B, J, EMBED), dtype=jnp.float32), 'Wq': jax.random.normal(ks[2], (EMBED, EMBED), dtype=jnp.float32) * s, 'bq': jnp.zeros((EMBED,), dtype=jnp.float32), 'Wk': jax.random.normal(ks[3], (EMBED, EMBED), dtype=jnp.float32) * s, 'bk': jnp.zeros((EMBED,), dtype=jnp.float32), 'Wv': jax.random.normal(ks[4], (EMBED, EMBED), dtype=jnp.float32) * s, 'bv': jnp.zeros((EMBED,), dtype=jnp.float32)}
    _L1_xattn_all = _L1_xattn_setup()
    _L1_xattn_in = {k: v for k, v in _L1_xattn_all.items() if k in ('Wq', 'bq', 'Wk', 'bk', 'Wv', 'bv')}
    del _L1_xattn_all

    def _L1_ffn_setup():
        import jax, jax.numpy as jnp
        import numpy as np
        DIM = 128
        HIDDEN = 384
        SCALE = 1.0 / 127.0

        def _dequant(w_int, dtype):
            return w_int.astype(dtype) * jnp.asarray(SCALE, dtype)
        key = jax.random.key(seed)
        k_x, k_g, k_u, k_d = jax.random.split(key, 4)
        x = jax.random.normal(k_x, (4, 256, DIM), dtype=jnp.float32)
        w_gate = jax.random.randint(k_g, (HIDDEN, DIM), -127, 128, dtype=jnp.int32)
        w_up = jax.random.randint(k_u, (HIDDEN, DIM), -127, 128, dtype=jnp.int32)
        w_down = jax.random.randint(k_d, (DIM, HIDDEN), -127, 128, dtype=jnp.int32)
        return {'x': x, 'w_gate': w_gate, 'w_up': w_up, 'w_down': w_down}
    _L1_ffn_all = _L1_ffn_setup()
    _L1_ffn_in = {k: v for k, v in _L1_ffn_all.items() if k in ('w_gate', 'w_up', 'w_down')}
    del _L1_ffn_all
    return {'x': x, 'ctx_1024': ctx_1024, 'L0_xattn_Wq': _L0_xattn_in['Wq'], 'L0_xattn_bq': _L0_xattn_in['bq'], 'L0_xattn_Wk': _L0_xattn_in['Wk'], 'L0_xattn_bk': _L0_xattn_in['bk'], 'L0_xattn_Wv': _L0_xattn_in['Wv'], 'L0_xattn_bv': _L0_xattn_in['bv'], 'L0_xattn_Wo': _L0_xattn_in['Wo'], 'L0_xattn_bo': _L0_xattn_in['bo'], 'L0_ffn_W1': _L0_ffn_in['W1'], 'L0_ffn_b1': _L0_ffn_in['b1'], 'L0_ffn_W2': _L0_ffn_in['W2'], 'L0_ffn_b2': _L0_ffn_in['b2'], 'L1_xattn_Wq': _L1_xattn_in['Wq'], 'L1_xattn_bq': _L1_xattn_in['bq'], 'L1_xattn_Wk': _L1_xattn_in['Wk'], 'L1_xattn_bk': _L1_xattn_in['bk'], 'L1_xattn_Wv': _L1_xattn_in['Wv'], 'L1_xattn_bv': _L1_xattn_in['bv'], 'L1_ffn_w_gate': _L1_ffn_in['w_gate'], 'L1_ffn_w_up': _L1_ffn_in['w_up'], 'L1_ffn_w_down': _L1_ffn_in['w_down']}

def reference(x, ctx_1024, L0_xattn_Wq, L0_xattn_bq, L0_xattn_Wk, L0_xattn_bk, L0_xattn_Wv, L0_xattn_bv, L0_xattn_Wo, L0_xattn_bo, L0_ffn_W1, L0_ffn_b1, L0_ffn_W2, L0_ffn_b2, L1_xattn_Wq, L1_xattn_bq, L1_xattn_Wk, L1_xattn_bk, L1_xattn_Wv, L1_xattn_bv, L1_ffn_w_gate, L1_ffn_w_up, L1_ffn_w_down):
    import jax
    import jax.numpy as jnp

    def _L0_xattn_ref(query, key_value, Wq, bq, Wk, bk, Wv, bv, Wo, bo):
        import jax, jax.numpy as jnp
        import numpy as np
        D_MODEL = 128
        NUM_HEADS = 16
        HEAD_DIM = D_MODEL // NUM_HEADS
        B, SQ, _ = query.shape
        SKV = key_value.shape[1]
        Q = query @ Wq.T + bq
        K = key_value @ Wk.T + bk
        V = key_value @ Wv.T + bv
        Q = Q.reshape(B, SQ, NUM_HEADS, HEAD_DIM).transpose(0, 2, 1, 3)
        K = K.reshape(B, SKV, NUM_HEADS, HEAD_DIM).transpose(0, 2, 1, 3)
        V = V.reshape(B, SKV, NUM_HEADS, HEAD_DIM).transpose(0, 2, 1, 3)
        scores = jnp.einsum('bhqd,bhkd->bhqk', Q, K) / np.sqrt(HEAD_DIM)
        causal = jnp.tril(jnp.ones((SQ, SKV), bool))
        scores = jnp.where(causal[None, None], scores, -jnp.inf)
        attn = jax.nn.softmax(scores, axis=-1)
        out = jnp.einsum('bhqk,bhkd->bhqd', attn, V)
        out = out.transpose(0, 2, 1, 3).reshape(B, SQ, D_MODEL)
        return out @ Wo.T + bo

    def _L0_ffn_ref(x, W1, b1, W2, b2):
        import jax, jax.numpy as jnp
        import numpy as np
        EPS = 1e-05

        def _quantize(W):
            gamma = jnp.mean(jnp.abs(W))
            return jnp.clip(jnp.round(W / (gamma + EPS)), -1.0, 1.0)
        Wq1 = _quantize(W1)
        Wq2 = _quantize(W2)
        h = jax.nn.relu(jnp.einsum('bsd,fd->bsf', x, Wq1) + b1)
        out = jnp.einsum('bsf,df->bsd', h, Wq2) + b2
        return out

    def _L1_xattn_ref(q_in, k_v, Wq, bq, Wk, bk, Wv, bv):
        import jax, jax.numpy as jnp
        import numpy as np
        EMBED = 128
        B, I, J = (8, 256, 256)
        SCALE = EMBED ** (-0.5)
        q = q_in @ Wq + bq
        k = k_v @ Wk + bk
        v = k_v @ Wv + bv
        sim = jnp.einsum('bid,bjd->bij', q, k) * SCALE
        attn = jax.nn.softmax(sim, axis=-1)
        out = jnp.einsum('bij,bjd->bid', attn, v)
        return out

    def _L1_ffn_ref(x, w_gate, w_up, w_down):
        import jax, jax.numpy as jnp
        import numpy as np
        DIM = 128
        HIDDEN = 384
        SCALE = 1.0 / 127.0

        def _dequant(w_int, dtype):
            return w_int.astype(dtype) * jnp.asarray(SCALE, dtype)
        wg = _dequant(w_gate, x.dtype)
        wu = _dequant(w_up, x.dtype)
        wd = _dequant(w_down, x.dtype)
        gate = jnp.einsum('bsd,hd->bsh', x, wg)
        up = jnp.einsum('bsd,hd->bsh', x, wu)
        h = jax.nn.silu(gate) * up
        return jnp.einsum('bsh,dh->bsd', h, wd)
    x = x + _L0_xattn_ref(_layernorm(x, axis=-1), ctx_1024, L0_xattn_Wq, L0_xattn_bq, L0_xattn_Wk, L0_xattn_bk, L0_xattn_Wv, L0_xattn_bv, L0_xattn_Wo, L0_xattn_bo)
    x = x + _L0_ffn_ref(_layernorm(x, axis=-1), L0_ffn_W1, L0_ffn_b1, L0_ffn_W2, L0_ffn_b2)
    x = x + _L1_xattn_ref(_layernorm(x, axis=-1), ctx_1024, L1_xattn_Wq, L1_xattn_bq, L1_xattn_Wk, L1_xattn_bk, L1_xattn_Wv, L1_xattn_bv)
    x = x + _L1_ffn_ref(_layernorm(x, axis=-1), L1_ffn_w_gate, L1_ffn_w_up, L1_ffn_w_down)
    return x

_drawn_inputs = setup_inputs


def setup_inputs(seed=0):
    import zlib

    import numpy as np

    out = dict(_drawn_inputs(seed))
    spreads = {'L0_xattn_bq': (0.0, 0.1),
     'L0_xattn_bk': (0.0, 2.0),
     'L0_xattn_bv': (0.0, 0.1),
     'L0_xattn_bo': (0.0, 0.1),
     'L1_xattn_bq': (0.0, 0.8),
     'L1_xattn_bk': (0.0, 2.0),
     'L1_xattn_bv': (0.0, 2.0)}
    factors = {'L0_ffn_b1': 7.451,
     'L0_ffn_b2': 200.0,
     'L1_xattn_Wq': 8.0,
     'L1_xattn_Wk': 8.0,
     'L1_xattn_Wv': 8.0}
    for name, (base, spread) in spreads.items():
        noise = np.random.default_rng([zlib.crc32(name.encode()), seed]).standard_normal(out[name].shape)
        drawn = base * np.exp(spread * noise) if base else spread * noise
        out[name] = jnp.asarray(drawn.astype(out[name].dtype))
    for name, factor in factors.items():
        out[name] = (out[name] * factor).astype(out[name].dtype)
    return out
```

```python
from contextlib import ExitStack

import numpy as np

import concourse.bass as bass
from concourse import mybir

F32 = mybir.dt.float32
F32R = mybir.dt.float32r
BF16 = mybir.dt.bfloat16
I32 = mybir.dt.int32
ALU = mybir.AluOpType
ACT = mybir.ActivationFunctionType
AX = mybir.AxisListType

P = 128
B, S, D = 4, 512, 128
TILES = S // P
KV = 77
H, HD = 16, 8
KP = 80
G = 4
HG = H // G
GK = HG * KP
CH = H * KP // P
HALF = CH // 2
KC = 2 * GK + P
VW = 2 * HG * (HD + 1)
F0 = 512 // P
F1 = 384 // P
EPS = 1e-5
NEG = -1e30
QSCALE = 1.0 / 127.0

EARLY = {"ctxp": B * 240, "wk0": G * 96, "wq0": P, "bq0": 1, "bk0": G, "headmask": HG,
         "lorows": 1, "ident": P}
LATE = {"wv0": P, "wo0": P, "w1": 512, "w2": 512, "b1": F0, "wk1": P, "wq1": P, "wv1": P,
        "bk1": 1, "bq1": 1, "vmask": CH * 8, "masks": GK, "maskt": CH * 78}
ROWS = {"bv0": P, "bo0": P, "b2": P, "bv1": P}
INTS = {"gate": 384, "up": 384, "down": 384}


def columns(widths):
    at, out = 0, {}
    for name, w in widths.items():
        out[name] = slice(at, at + w)
        at += w
    return out, at


class Ring:

    def __init__(self, banks, full, freed, keys):
        self.banks, self.full, self.freed = banks, full, freed
        self.at = {k: n for n, k in enumerate(keys)}
        assert len(self.at) == len(keys)

    def bank(self, key):
        return self.banks[self.at[key] % len(self.banks)]

    def freed_sem(self, key):
        return self.freed[self.at[key] % len(self.banks)]

    def claim(self, eng, key):
        n = self.at[key] // len(self.banks)
        if n:
            eng.wait_ge(self.freed_sem(key), n)

    def wait_full(self, eng, key):
        eng.wait_ge(self.full, self.at[key] + 1)

    def wait_taken(self, eng, key):
        eng.wait_ge(self.freed_sem(key), self.at[key] // len(self.banks) + 1)


def tensor_steps():
    s = [("xT", 0, 0), ("q", 0), ("k0",), ("xT", 0, 1), ("q", 1), ("s", 0), ("v0",), ("gamma",),
         ("xT", 0, 2), ("q", 2), ("m", 0), ("s+p", 0), ("av", 0, 0), ("m", 1), ("av", 0, 1),
         ("xT", 0, 3), ("q", 3), ("y0", 0),
         ("s+p", 1), ("av", 1, 0), ("m", 2), ("av", 1, 1), ("y0", 1),
         ("s+p", 2), ("av", 2, 0), ("m", 3), ("av", 2, 1), ("y0", 2),
         ("p", 3), ("kv1",), ("xT", 1, 0), ("av", 3, 0), ("av", 3, 1), ("y0", 3), ("xT", 1, 1)]
    s += [("h", 0), ("xT", 1, 2), ("h", 1), ("y1", 0), ("xT", 1, 3), ("h", 2), ("y1", 1),
          ("h", 3), ("y1", 2), ("xT", 2, 0), ("sim", 0), ("y1", 3)]
    s += [("xT", 2, 1), ("sim", 1), ("y2", 0), ("xT", 2, 2), ("sim", 2), ("y2", 1),
          ("xT", 2, 3), ("sim", 3), ("y2", 2), ("xT", 3, 0), ("gu", 0), ("y2", 3)]
    s += [("xT", 3, 1), ("gu", 1), ("y3", 0), ("xT", 3, 2), ("gu", 2), ("y3", 1),
          ("xT", 3, 3), ("gu", 3), ("y3", 2), ("y3", 3)]
    return s


def s_units():
    return [(t, g) for t in range(TILES) for g in range(G)]


def mixed_units():
    su, out = s_units(), []
    for c in range(CH):
        out.append(("p", c))
        for _ in range(2 if c < 6 else 1):
            out.append(("s", su.pop(0)))
    assert not su
    return out


def ring_keys(steps):
    t, s, e = [], [], []
    for st in steps:
        k = st[0]
        if k in ("xT", "q", "m", "av", "kv1", "sim", "gamma"):
            if k == "kv1":
                t += [("k1",), ("kq",), ("bq",), ("v1",)]
            else:
                t.append(st)
        elif k == "k0":
            e += [("k0", g) for g in range(G)]
        elif k == "v0":
            e += [("v0", b, u) for b in range(B) for u in range(2)]
        elif k == "s":
            s += [("s", st[1], tt, g) for tt, g in s_units()]
        elif k == "p":
            e += [("p", st[1], c) for c in range(CH)]
        elif k == "s+p":
            s += [("s", st[1] + 1, tt, g) for tt, g in s_units()]
            e += [("p", st[1], c) for c in range(CH)]
        elif k == "y0":
            t += [("oT", st[1]), ("y", 0, st[1])]
        elif k == "h":
            e += [("h", st[1], f) for f in range(0, F0, 2)]
            s += [("h", st[1], f) for f in range(1, F0, 2)]
        elif k == "y2":
            t += [("pT", st[1]), ("y", 2, st[1])]
        elif k in ("y1", "y3"):
            t.append(("y", int(k[1]), st[1]))
        elif k == "gu":
            e += [("gate", st[1], f) for f in range(F1)]
            s += [("up", st[1], f) for f in range(F1)]
    return t, s, e


def build(nc, x, early, late, rows, ints, selector, out):
    ec, en = columns(EARLY)
    lc, ln_ = columns(LATE)
    rc, rn = columns(ROWS)
    ic, inn = columns(INTS)
    steps = tensor_steps()
    x_dram = x.rearrange("(b t p) d -> b p t d", b=B, p=P)
    out_dram = out.rearrange("(b t p) d -> b p t d", b=B, p=P)

    with ExitStack() as ctx:
        def sb(name, shape, dt=F32):
            return ctx.enter_context(nc.sbuf_tensor(name, shape, dt))

        def sem(name):
            return ctx.enter_context(nc.semaphore(name))

        def ring(name, n, keys):
            banks = [ctx.enter_context(nc.psum_tensor(f"{name}{i}", [P, 512], F32)) for i in range(n)]
            return Ring(banks, sem(f"{name}_full"), [sem(f"{name}_freed{i}") for i in range(n)], keys)

        tk, sk, ek = ring_keys(steps)
        T = ring("turn", 2, tk)
        SR = ring("score", 3, sk)
        ER = ring("exp", 3, ek)

        ew = sb("early_sb", [P, en])
        lw = sb("late_sb", [P, ln_])
        rw = sb("rows_sb", [P, rn])
        iw = sb("ints_sb", [P, inn], I32)
        E = {n: ew[:, c] for n, c in ec.items()}
        L = {n: lw[:, c] for n, c in lc.items()}
        R = {n: rw[:, c] for n, c in rc.items()}
        ctxp = E["ctxp"].rearrange("p (b c) -> p b c", b=B)
        ident = E["ident"]
        w1q = sb("w1_ternary", [P, 512], F32R)
        w2q = sb("w2_ternary", [P, 512])
        gu_w = sb("gate_up_w", [P, 768], F32R)
        down_w = sb("down_w", [P, 384])
        ident16 = sb("ident16", [P, P], BF16)
        masks16 = sb("mask_scores", [P, GK], BF16)
        maskt16 = sb("mask_scoresT", [P, CH * 78], BF16)
        ones = sb("ones", [P, P])
        half = sb("minus_half", [P, TILES])
        gsum = sb("abs_sums", [P, 2])
        thr = sb("threshold", [P, 4])
        kst = sb("k0_stack", [P, B, 2, KC], F32R)
        vt = sb("v0_rows", [P, 2, 320])
        vx = sb("v0_block", [P, B, CH, VW])
        k1 = sb("k1T", [P, B * KV])
        kq = sb("wq_k1", [P, B * KV])
        bqb = sb("bq1_columns", [P, P])
        bqk = sb("bq1_k1", [P, B * KV])
        v1 = sb("v1", [KV, B, D])
        xs = sb("x_sb", [P, B, TILES, D])
        xb = sb("x_bias", [P, B, TILES, D])
        xh = sb("x_hat", [P, B, TILES, D])
        xt = sb("x_hatT", [P, B, S])
        hi = sb("hi", [P, B, S], F32R)
        lo = sb("lo", [P, B, S], F32R)
        stats = sb("bn_stats", [P, B, TILES, 6])
        mv = sb("mean_var", [P, B, TILES, 2])
        ve = sb("var_eps", [P, B, TILES])
        rstd = sb("rstd", [P, B, TILES])
        qst = sb("q_stack", [P, 2, G, S], F32R)
        mx = sb("max0", [P, B, TILES, H])
        mhl = sb("max0_hi_lo", [P, B, TILES, 2 * H])
        mrow = sb("max0_rows", [2 * H, B, S], F32R)
        pr = sb("probs0", [P, 2, CH, S])
        rs = sb("rsum0", [P, B, 2, 32])
        at0 = sb("attn0", [P, 2, TILES, D])
        at0T = sb("attn0T", [P, 2, S])
        m1 = sb("max1", [P, B, TILES])
        s1 = sb("sum1", [P, B, TILES])
        r1 = sb("rsum1", [P, B, TILES])
        prf = pr[:].rearrange("p s c q -> p (s c q)")
        kf = prf[0:96, 0:G * B * KV]
        khi = prf[0:96, G * B * KV:2 * G * B * KV].bitcast(F32R)
        wtmp = pr[:, 1, CH - 1]
        hT = pr[:, :, 0:F0]
        sg = pr[:, 0, F0:F0 + 3]
        p1T = pr[0:KV, :, F0 + 3]
        sm = pr[:, :, F0 + 4, 0:TILES * KV].rearrange("p s (t k) -> p s t k", t=TILES)
        p1 = pr[:, :, F0 + 5, 0:TILES * KV].rearrange("p s (t k) -> p s t k", t=TILES)

        early_in, late_in, rows_in, ints_in = sem("early_in"), sem("late_in"), sem("rows_in"), sem("ints_in")
        x_in = [sem(f"x_in{b}") for b in range(B)]
        sel_in = sem("selector_in")
        q_in = [sem(f"q_stack_in{b}") for b in range(B)]
        m_in = [sem(f"max_rows_in{b}") for b in range(B)]
        out_done = sem("out_done")
        ln_stats, ln_mv, ln_ve, ln_rstd, ln_xh = (sem(n) for n in ("ln_stats", "ln_mv", "ln_ve", "ln_rstd", "ln_xhat"))
        hi_done = sem("hi_done")
        bias_done = sem("bias_done")
        consts = sem("consts_done")
        kzero = sem("k_stack_zeroed")
        dprep = sem("vector_prep")
        kparts = sem("k_parts")
        vrows = sem("v_rows")
        vblock = sem("v_block")
        wq_done = sem("ternary_done")
        i_done = sem("int_weights_done")
        bq_done = sem("bq_columns_done")
        mhi_done, mhl_done = sem("max_hi_done"), sem("max_hi_lo_done")
        rs_done = sem("rsum0_done")
        sim_add, sim_max, sim_sub, p1_done, s1_done, r1_done = (
            sem(n) for n in ("sim_added", "sim_max", "sim_shifted", "probs1_done", "sum1_done", "rsum1_done"))
        masked_first = sem("masked_first")
        half_done, cast_done = sem("minus_half_done"), sem("cast_done")

        block = ctx.enter_context(nc.Block())

        hi_order = [("q", b) for b in range(B)] + [("x", 1, b) for b in range(B)] + [("x", 3, b) for b in range(B)]
        hi_at = {k: n + 1 for n, k in enumerate(hi_order)}

        @block.sync
        def _(sp):
            sp.dma_start(xs[:, 0], x_dram[0]).then_inc(x_in[0], 16)
            sp.dma_start(ew[:], early).then_inc(early_in, 16)
            for b in range(1, B):
                sp.dma_start(xs[:, b], x_dram[b]).then_inc(x_in[b], 16)
            sp.dma_start(lw[:], late).then_inc(late_in, 16)
            sp.dma_start(rw[:], rows.partition_broadcast(P)).then_inc(rows_in, 16)
            sp.dma_start(iw[:], ints).then_inc(ints_in, 16)

            def stack_q(b):
                if b >= 2:
                    ER.wait_taken(sp, ("p", b - 2, CH - 1))
                sp.wait_ge(hi_done, hi_at["q", b])
                for part in range(2):
                    for g in range(G):
                        sp.dma_start(qst[32 * part:32 * part + 32, b % 2, g].bitcast(F32),
                                     hi[32 * g:32 * g + 32, b].bitcast(F32)).then_inc(q_in[b], 16)
                T.wait_taken(sp, ("q", b))
                for g in range(G):
                    sp.dma_start(qst[64:96, b % 2, g].bitcast(F32),
                                 lo[32 * g:32 * g + 32, b].bitcast(F32)).then_inc(q_in[b], 16)

            def stack_max(b):
                if b >= 2:
                    ER.wait_taken(sp, ("p", b - 2, CH - 1))
                T.wait_taken(sp, ("m", b))
                for g in range(G):
                    sp.dma_start(qst[96:128, b % 2, g].bitcast(F32),
                                 mrow[:, b].bitcast(F32)).then_inc(m_in[b], 16)

            stack_q(0)
            stack_q(1)
            stack_max(0)
            stack_q(2)
            stack_max(1)
            stack_q(3)
            stack_max(2)
            stack_max(3)
            for b in range(B):
                T.wait_taken(sp, ("y", 3, b))
                sp.dma_start(out_dram[b], xs[:, b]).then_inc(out_done, 16)
            sp.wait_ge(out_done, 16 * B)

        @block.tensor
        def _(pe):
            def turn_x(l, b):
                key = ("xT", l, b)
                T.claim(pe, key)
                if l == 0 and b == 0:
                    pe.wait_ge(early_in, 16)
                pe.wait_ge(ln_xh, B * l + b + 1)
                for t in range(TILES):
                    last = nc.tensor.transpose(T.bank(key)[:, t * P:(t + 1) * P], xh[:, b, t], ident)
                last.then_inc(T.full, 1)

            def project_q(b):
                T.claim(pe, ("q", b))
                T.wait_taken(pe, ("xT", 0, b))
                nc.tensor.matmul(T.bank(("q", b))[:], E["wq0"], xt[:, b], start=True, stop=True).then_inc(T.full, 1)

            def keys0():
                for g in range(G):
                    ER.claim(pe, ("k0", g))
                    nc.tensor.matmul(ER.bank(("k0", g))[0:96, 0:B * KV].rearrange("p (b k) -> p b k", b=B),
                                     E["wk0"][:, g * 96:(g + 1) * 96], ctxp[:, :, 0:KV],
                                     start=True, stop=True).then_inc(ER.full, 1)

            def values0():
                pe.wait_ge(late_in, 16)
                for b in range(B):
                    for u in range(2):
                        key = ("v0", b, u)
                        ER.claim(pe, key)
                        for c in range(HALF):
                            off = (P * c) % KP
                            last = nc.tensor.matmul(ER.bank(key)[:, 64 * c:64 * c + 64], ctxp[:, b, off:off + P],
                                                    L["wv0"][:, 64 * u:64 * u + 64], start=True, stop=True)
                        last.then_inc(ER.full, 1)

            def gamma():
                T.claim(pe, ("gamma",))
                pe.wait_ge(consts, 1)
                pe.wait_ge(dprep, 2)
                nc.tensor.matmul(T.bank(("gamma",))[:, 0:2], ones[:], gsum[:], start=True, stop=True).then_inc(T.full, 1)

            def scores(b, t, g):
                key = ("s", b, t, g)
                SR.claim(pe, key)
                o = SR.bank(key)[:, 0:GK]
                kcol = (g % 2) * (GK + P)
                nc.tensor.matmul(o, qst[0:96, b % 2, g, t * P:(t + 1) * P], kst[0:96, b, g // 2, kcol:kcol + GK],
                                 start=True, stop=t > 0).then_inc(*((SR.full, 1) if t else (masked_first, 1)))
                if t == 0:
                    nc.tensor.matmul(o, ident16[:], masks16[:], start=False, stop=True).then_inc(SR.full, 1)

            def scores_begin(b):
                pe.wait_ge(q_in[b], 16 * 3 * G)
                if b == 0:
                    pe.wait_ge(kparts, 4)
                    pe.wait_ge(consts, 2)

            def scores_t(b, c):
                key = ("p", b, c)
                ER.claim(pe, key)
                o = ER.bank(key)[:]
                u, i = divmod(c, HALF)
                parts = {0: [(0, 0)], 1: [(P, 0)], 2: [(2 * P, 0), (3 * P, 1)], 3: [(4 * P, 1)], 4: [(5 * P, 1)]}[i]
                for n, (col, g) in enumerate(parts):
                    nc.tensor.matmul(o, kst[:, b, u, col:col + P], qst[:, b % 2, 2 * u + g],
                                     start=n == 0, stop=n == len(parts) - 1)
                nc.tensor.matmul(o[:, 0:78], ident16[:], maskt16[:, 78 * c:78 * c + 78],
                                 start=False, stop=True, skip_group_check=True).then_inc(ER.full, 1)

            def scores_t_begin(b):
                pe.wait_ge(m_in[b], 16 * G)
                if b == 0:
                    pe.wait_ge(sel_in, 16 * B)

            def turn_max(b):
                key = ("m", b)
                T.claim(pe, key)
                pe.wait_ge(mhl_done, b + 1)
                for t in range(TILES):
                    last = nc.tensor.transpose(T.bank(key)[0:2 * H, t * P:(t + 1) * P], mhl[:, b, t], ident)
                last.then_inc(T.full, 1)

            def attend(b, pair):
                key = ("av", b, pair)
                T.claim(pe, key)
                if pair == 0:
                    for c in range(CH - 3, CH):
                        ER.wait_taken(pe, ("p", b, c))
                    if b == 0:
                        pe.wait_ge(vblock, 2 * B + 1)
                n = 0
                for t2 in range(2):
                    for u in range(2):
                        for c in range(HALF):
                            col = (t2 * 2 + u) * VW
                            last = nc.tensor.matmul(
                                T.bank(key)[:, col:col + VW],
                                pr[:, b % 2, u * HALF + c, (2 * pair + t2) * P:(2 * pair + t2 + 1) * P],
                                vx[:, b, u * HALF + c], start=n == 0, stop=n == 19, skip_group_check=True)
                            n += 1
                last.then_inc(T.full, 1)

            def turn_attended(b):
                key = ("oT", b)
                T.claim(pe, key)
                for pair in range(2):
                    T.wait_taken(pe, ("av", b, pair))
                for t in range(TILES):
                    last = nc.tensor.transpose(T.bank(key)[:, t * P:(t + 1) * P], at0[:, b % 2, t], ident)
                last.then_inc(T.full, 1)

            def output(l, b, lhs, rhs):
                key = ("y", l, b)
                T.claim(pe, key)
                n = len(rhs)
                for t in range(TILES):
                    for f in range(n):
                        last = nc.tensor.matmul(T.bank(key)[:, t * P:(t + 1) * P], lhs(f, t), rhs[f],
                                                start=f == 0, stop=f == n - 1)
                last.then_inc(T.full, 1)

            def hidden0(b):
                T.wait_taken(pe, ("xT", 1, b))
                if b == 0:
                    pe.wait_ge(wq_done, 2)
                for f in range(F0):
                    ring_ = SR if f % 2 else ER
                    key = ("h", b, f)
                    ring_.claim(pe, key)
                    nc.tensor.matmul(ring_.bank(key)[:], w1q[:, f * P:(f + 1) * P], hi[:, b], start=True, stop=False)
                    nc.tensor.matmul(ring_.bank(key)[:], w1q[:, f * P:(f + 1) * P], lo[:, b],
                                     start=False, stop=True).then_inc(ring_.full, 1)

            def keys_values1():
                cols = ctxp[:, :, 0:KV]
                T.claim(pe, ("k1",))
                nc.tensor.matmul(T.bank(("k1",))[:, 0:B * KV].rearrange("p (b k) -> p b k", b=B), L["wk1"], cols,
                                 start=True, stop=True).then_inc(T.full, 1)
                T.wait_taken(pe, ("k1",))
                T.claim(pe, ("kq",))
                nc.tensor.matmul(T.bank(("kq",))[:, 0:B * KV], L["wq1"], k1[:], start=True, stop=True).then_inc(T.full, 1)
                T.claim(pe, ("bq",))
                pe.wait_ge(bq_done, 1)
                nc.tensor.matmul(T.bank(("bq",))[:, 0:B * KV], bqb[:], k1[:], start=True, stop=True).then_inc(T.full, 1)
                T.claim(pe, ("v1",))
                for b in range(B):
                    last = nc.tensor.matmul(T.bank(("v1",))[0:KV, b * D:(b + 1) * D], ctxp[:, b, 0:KV], L["wv1"],
                                            start=True, stop=True)
                last.then_inc(T.full, 1)

            def sim1(b):
                key = ("sim", b)
                T.claim(pe, key)
                T.wait_taken(pe, ("xT", 2, b))
                if b == 0:
                    T.wait_taken(pe, ("kq",))
                for t in range(TILES):
                    last = nc.tensor.matmul(T.bank(key)[:, t * KV:(t + 1) * KV], xt[:, b, t * P:(t + 1) * P],
                                            kq[:, b * KV:(b + 1) * KV], start=True, stop=True)
                last.then_inc(T.full, 1)

            def turn_probs1(b):
                key = ("pT", b)
                T.claim(pe, key)
                pe.wait_ge(p1_done, b + 1)
                for t in range(TILES):
                    last = nc.tensor.transpose(T.bank(key)[0:KV, t * P:(t + 1) * P], p1[:, b % 2, t], ident)
                last.then_inc(T.full, 1)

            def gate_up(b):
                T.wait_taken(pe, ("xT", 3, b))
                if b == 0:
                    pe.wait_ge(i_done, 3)
                for f in range(F1):
                    for ring_, key, col in ((ER, ("gate", b, f), 0), (SR, ("up", b, f), 384)):
                        ring_.claim(pe, key)
                        w = gu_w[:, col + f * P:col + (f + 1) * P]
                        nc.tensor.matmul(ring_.bank(key)[:], w, hi[:, b], start=True, stop=False)
                        nc.tensor.matmul(ring_.bank(key)[:], w, lo[:, b], start=False, stop=True).then_inc(ring_.full, 1)

            for st in steps:
                k = st[0]
                b = st[-1]
                if k == "xT":
                    turn_x(st[1], b)
                elif k == "q":
                    project_q(b)
                elif k == "k0":
                    keys0()
                elif k == "v0":
                    values0()
                elif k == "gamma":
                    gamma()
                elif k == "s":
                    scores_begin(b)
                    for t, g in s_units():
                        scores(b, t, g)
                elif k == "m":
                    turn_max(b)
                elif k == "s+p":
                    scores_t_begin(b)
                    scores_begin(b + 1)
                    for kind, unit in mixed_units():
                        if kind == "p":
                            scores_t(b, unit)
                        else:
                            scores(b + 1, *unit)
                elif k == "p":
                    scores_t_begin(b)
                    for c in range(CH):
                        scores_t(b, c)
                elif k == "av":
                    attend(st[1], st[2])
                elif k == "y0":
                    turn_attended(b)
                    T.wait_taken(pe, ("oT", b))
                    output(0, b, lambda f, t: at0T[:, b % 2, t * P:(t + 1) * P], [L["wo0"]])
                elif k == "kv1":
                    keys_values1()
                elif k == "h":
                    hidden0(b)
                elif k == "y1":
                    for f in range(F0):
                        (SR if f % 2 else ER).wait_taken(pe, ("h", b, f))
                    output(1, b, lambda f, t: hT[:, b % 2, f, t * P:(t + 1) * P],
                           [w2q[:, f * P:(f + 1) * P] for f in range(F0)])
                elif k == "sim":
                    sim1(b)
                elif k == "y2":
                    turn_probs1(b)
                    T.wait_taken(pe, ("pT", b))
                    if b == 0:
                        T.wait_taken(pe, ("v1",))
                    output(2, b, lambda f, t: p1T[:, b % 2, t * P:(t + 1) * P], [v1[:, b]])
                elif k == "gu":
                    gate_up(b)
                elif k == "y3":
                    for f in range(F1):
                        SR.wait_taken(pe, ("up", b, f))
                    output(3, b, lambda f, t: hT[:, b % 2, f, t * P:(t + 1) * P],
                           [down_w[:, f * P:(f + 1) * P] for f in range(F1)])

        @block.scalar
        def _(act):
            def copy_bank(key, dst, parts=P):
                T.wait_full(act, key)
                nc.scalar.activation(dst, T.bank(key)[0:parts, :], ACT.Copy).then_inc(T.freed_sem(key), 1)

            def x_hi(l, b):
                T.wait_full(act, ("xT", l, b))
                nc.scalar.activation(hi[:, b], T.bank(("xT", l, b))[:], ACT.Copy).then_inc(hi_done, 1)

            def q_hi(b):
                T.wait_full(act, ("q", b))
                nc.scalar.activation(hi[:, b], T.bank(("q", b))[:], ACT.Identity, bias=E["bq0"]).then_inc(hi_done, 1)

            def exps(b):
                for c in range(CH):
                    key = ("p", b, c)
                    ER.wait_full(act, key)
                    if b >= 2 and c == 0:
                        T.wait_taken(act, ("av", b - 2, 1))
                    nc.scalar.activation(pr[:, b % 2, c], ER.bank(key)[:], ACT.Exp,
                                         scale=HD ** -0.5).then_inc(ER.freed_sem(key), 1)

            def relu(b):
                for f in range(0, F0, 2):
                    key = ("h", b, f)
                    ER.wait_full(act, key)
                    if b >= 2 and f == 0:
                        T.wait_full(act, ("y", 1, b - 2))
                    nc.scalar.activation(hT[:, b % 2, f], ER.bank(key)[:], ACT.Relu,
                                         bias=L["b1"][:, f:f + 1]).then_inc(ER.freed_sem(key), 1)

            def exp1(b):
                act.wait_ge(sim_sub, b + 1)
                if b >= 2:
                    T.wait_full(act, ("pT", b - 2))
                    act.wait_ge(s1_done, b - 1)
                nc.scalar.activation(p1[:, b % 2], sm[:, b % 2], ACT.Exp, scale=D ** -0.5).then_inc(p1_done, 1)

            def silu(b):
                for f in range(F1):
                    key = ("gate", b, f)
                    ER.wait_full(act, key)
                    n = b * F1 + f
                    if n >= 3:
                        SR.wait_taken(act, ("up", *divmod(n - 3, F1)))
                    nc.scalar.activation(sg[:, n % 3], ER.bank(key)[:], ACT.Silu,
                                         scale=QSCALE).then_inc(ER.freed_sem(key), 1)

            def take_x(b):
                copy_bank(("xT", 0, b), xt[:, b])
                if b == 0:
                    act.wait_ge(early_in, 16)
                q_hi(b)

            def take_max(b):
                copy_bank(("m", b), mrow[:, b], 2 * H)

            take_x(0)
            take_x(1)
            take_x(2)
            take_max(0)
            exps(0)
            take_max(1)
            take_x(3)
            copy_bank(("oT", 0), at0T[:, 0])
            exps(1)
            take_max(2)
            copy_bank(("oT", 1), at0T[:, 1])
            exps(2)
            take_max(3)
            copy_bank(("oT", 2), at0T[:, 0])
            exps(3)
            x_hi(1, 0)
            copy_bank(("oT", 3), at0T[:, 1])
            x_hi(1, 1)
            act.wait_ge(late_in, 16)
            relu(0)
            x_hi(1, 2)
            relu(1)
            x_hi(1, 3)
            relu(2)
            relu(3)
            copy_bank(("xT", 2, 0), xt[:, 0])
            exp1(0)
            for b in range(1, B):
                copy_bank(("xT", 2, b), xt[:, b])
                T.wait_full(act, ("pT", b - 1))
                if b >= 3:
                    T.wait_full(act, ("y", 2, b - 3))
                nc.scalar.activation(p1T[:, (b - 1) % 2], T.bank(("pT", b - 1))[0:KV, :],
                                     ACT.Copy).then_inc(T.freed_sem(("pT", b - 1)), 1)
                exp1(b)
            x_hi(3, 0)
            silu(0)
            T.wait_full(act, ("pT", 3))
            T.wait_full(act, ("y", 2, 1))
            nc.scalar.activation(p1T[:, 1], T.bank(("pT", 3))[0:KV, :], ACT.Copy).then_inc(T.freed_sem(("pT", 3)), 1)
            for b in range(1, B):
                x_hi(3, b)
                silu(b)

        @block.gpsimd
        def _(pool):
            nc.gpsimd.memset(kst[0:96].bitcast(F32), 0.0).then_inc(kzero, 1)
            for b in range(B):
                pool.dma_start(kst[96:128, b].rearrange("p u c -> p (u c)"), selector).then_inc(sel_in, 16)
            nc.gpsimd.memset(half[:], -0.5).then_inc(half_done, 1)

            def rstd_of(l, b):
                n = B * l + b
                pool.wait_ge(ln_mv, n + 1)
                nc.gpsimd.tensor_scalar(ve[:, b], mv[:, b, :, 1], EPS, None, ALU.add).then_inc(ln_ve, 1)
                pool.wait_ge(ln_ve, n + 1)
                nc.gpsimd.tensor_tensor(rstd[:, b], ve[:, b], half[:], ALU.pow).then_inc(ln_rstd, 1)

            def add_bias(l, b):
                if l == 0:
                    pool.wait_ge(x_in[b], 16)
                    pool.wait_ge(rows_in, 16)
                else:
                    T.wait_taken(pool, ("y", l - 1, b))
                bias = R["bo0"] if l == 0 else R["b2"]
                nc.gpsimd.tensor_tensor(xb[:, b], xs[:, b], bias.unsqueeze(1).broadcast_to([P, TILES, D]),
                                        ALU.add).then_inc(bias_done, 1)

            pool.wait_ge(half_done, 1)
            rstd_of(0, 0)
            nc.gpsimd.memset(ones[:], 1.0).then_inc(consts, 1)
            rstd_of(0, 1)
            pool.wait_ge(late_in, 16)
            pool.wait_ge(consts, 1)
            nc.gpsimd.tensor_copy(ident16[:], ident)
            nc.gpsimd.tensor_copy(masks16[:], L["masks"]).then_inc(cast_done, 1)
            rstd_of(0, 2)
            nc.gpsimd.tensor_copy(maskt16[:], L["maskt"]).then_inc(cast_done, 1)
            pool.wait_ge(cast_done, 2)
            nc.gpsimd.memset(bqb[:], 0.0).then_inc(consts, 1)
            vxv = vx[:].rearrange("p b (u c) (h e) -> p b u c h e", u=2, e=HD + 1)
            vm = L["vmask"].rearrange("p (u c h) -> p u c h", u=2, c=HALF)
            for b in range(B):
                for u in range(2):
                    n = 2 * b + u
                    ER.wait_taken(pool, ("v0", b, u))
                    v = vt[:, u].rearrange("p (c h e) -> p c h e", c=HALF, e=HD)
                    for c in range(HALF):
                        last = nc.gpsimd.tensor_tensor(vxv[:, b, u, c, :, 0:HD], v[:, c],
                                                       vm[:, u, c].unsqueeze(2).broadcast_to([P, 8, HD]), ALU.mult)
                    last.then_inc(vblock, 1)
            for b in range(B):
                last = nc.gpsimd.tensor_copy(vx[:, b].rearrange("p c (h e) -> p (c h) e", e=HD + 1)[:, :, HD],
                                             L["vmask"])
            last.then_inc(vblock, 1)
            rstd_of(0, 3)
            pool.wait_ge(consts, 2)
            nc.gpsimd.tensor_scalar(bqb[:], bqb[:], L["bq1"], None, ALU.add).then_inc(bq_done, 1)
            for b in range(B):
                add_bias(0, b)
            pool.wait_ge(ints_in, 16)
            nc.gpsimd.tensor_copy(gu_w[:, 0:384], iw[:, ic["gate"]]).then_inc(i_done, 1)
            nc.gpsimd.tensor_copy(gu_w[:, 384:768], iw[:, ic["up"]]).then_inc(i_done, 1)
            nc.gpsimd.tensor_copy(down_w[:], iw[:, ic["down"]]).then_inc(i_done, 1)
            for b in range(B):
                rstd_of(1, b)
                add_bias(1, b)
            for l in (2, 3):
                for b in range(B):
                    rstd_of(l, b)

        @block.vector
        def _(dve):
            def ln_begin(l, b):
                n = B * l + b
                if l == 0:
                    dve.wait_ge(x_in[b], 16)
                else:
                    T.wait_taken(dve, ("y", l - 1, b))
                for t in range(TILES):
                    last = nc.vector.bn_stats(stats[:, b, t], xs[:, b, t])
                last.then_inc(ln_stats, 1)
                dve.wait_ge(ln_stats, n + 1)
                for t in range(TILES):
                    last = nc.vector.bn_aggr(mv[:, b, t], stats[:, b, t])
                last.then_inc(ln_mv, 1)

            def ln_end(l, b):
                dve.wait_ge(ln_rstd, B * l + b + 1)
                for t in range(TILES):
                    last = nc.vector.tensor_scalar(xh[:, b, t], xs[:, b, t], mv[:, b, t, 0:1],
                                                   rstd[:, b, t:t + 1], ALU.subtract, ALU.mult)
                last.then_inc(ln_xh, 1)

            def q_lo(b):
                dve.wait_ge(hi_done, hi_at["q", b])
                nc.vector.scalar_tensor_tensor(lo[:, b], T.bank(("q", b))[:], E["bq0"], hi[:, b].bitcast(F32),
                                               ALU.add, ALU.subtract).then_inc(T.freed_sem(("q", b)), 1)

            def x_lo(l, b):
                dve.wait_ge(hi_done, hi_at["x", l, b])
                nc.vector.tensor_tensor(lo[:, b], T.bank(("xT", l, b))[:], hi[:, b].bitcast(F32),
                                        ALU.subtract).then_inc(T.freed_sem(("xT", l, b)), 1)

            def keys0():
                dve.wait_ge(early_in, 16)
                w = B * KV
                for g in range(G):
                    ER.wait_full(dve, ("k0", g))
                    nc.vector.tensor_scalar(kf[:, g * w:(g + 1) * w], ER.bank(("k0", g))[0:96, 0:w],
                                            E["bk0"][0:96, g:g + 1], None, ALU.add).then_inc(ER.freed_sem(("k0", g)), 1)
                ER.wait_taken(dve, ("k0", 1))
                ER.wait_taken(dve, ("k0", 2))
                ER.wait_taken(dve, ("k0", 3))
                nc.vector.tensor_copy(khi, kf).then_inc(kparts, 1)
                dve.wait_ge(kparts, 1)
                nc.vector.scalar_tensor_tensor(kf, khi.bitcast(F32), E["lorows"][0:96], kf,
                                               ALU.mult, ALU.add).then_inc(kparts, 1)
                dve.wait_ge(kparts, 2)
                dve.wait_ge(kzero, 1)
                for g in range(G):
                    src = kf[:, g * w:(g + 1) * w].rearrange("p (b k) -> p b k", b=B)
                    for j in range(HG):
                        col = (g % 2) * (GK + P) + j * KP
                        last = nc.vector.tensor_scalar(kst[0:96, :, g // 2, col:col + KV], src,
                                                       E["headmask"][0:96, j:j + 1], None, ALU.mult)
                last.then_inc(kparts, 2)

            def values0():
                dve.wait_ge(rows_in, 16)
                for b in range(B):
                    for u in range(2):
                        key = ("v0", b, u)
                        ER.wait_full(dve, key)
                        if b:
                            dve.wait_ge(vblock, 2 * b + u - 1)
                        bias = R["bv0"][:, 64 * u:64 * u + 64].unsqueeze(1).broadcast_to([P, HALF, 64])
                        nc.vector.tensor_tensor(vt[:, u].rearrange("p (c e) -> p c e", c=HALF),
                                                ER.bank(key)[:, 0:320].rearrange("p (c e) -> p c e", c=HALF),
                                                bias, ALU.add).then_inc(ER.freed_sem(key), 1)

            def abs_sums():
                dve.wait_ge(late_in, 16)
                for i, name in enumerate(("w1", "w2")):
                    nc.vector.tensor_reduce(gsum[:, i:i + 1], L[name], AX.X, ALU.add,
                                            apply_absolute_value=True).then_inc(dprep, 1)

            def ternary():
                T.wait_full(dve, ("gamma",))
                n = float(512 * 128)
                g = T.bank(("gamma",))
                nc.vector.tensor_scalar(thr[:, 0:2], g[:, 0:2], 0.5 / n, 0.5 * EPS, ALU.mult, ALU.add)
                nc.vector.tensor_scalar(thr[:, 2:4], g[:, 0:2], -0.5 / n, -0.5 * EPS, ALU.mult,
                                        ALU.add).then_inc(T.freed_sem(("gamma",)), 1)
                T.wait_taken(dve, ("gamma",))
                for i, (name, dst) in enumerate((("w1", w1q), ("w2", w2q))):
                    if i:
                        dve.wait_ge(wq_done, 1)
                    nc.vector.tensor_scalar(wtmp, L[name], thr[:, 2 + i:3 + i], None, ALU.is_lt).then_inc(dprep, 1)
                    dve.wait_ge(dprep, 3 + i)
                    nc.vector.scalar_tensor_tensor(dst[:], L[name], thr[:, i:i + 1], wtmp, ALU.is_gt,
                                                   ALU.subtract).then_inc(wq_done, 1)

            def maxima(b, t, g):
                key = ("s", b, t, g)
                SR.wait_full(dve, key)
                s_ = SR.bank(key)[:, 0:GK].rearrange("p (h k) -> p h k", h=HG)
                nc.vector.tensor_reduce(mx[:, b, t, HG * g:HG * g + HG], s_[:, :, 0:KV], AX.X,
                                        ALU.max).then_inc(SR.freed_sem(key), 1)

            def max_parts(b):
                for u in s_units()[-3:]:
                    SR.wait_taken(dve, ("s", b, *u))
                nc.vector.tensor_copy(mhl[:, b, :, 0:H].bitcast(F32R), mx[:, b]).then_inc(mhi_done, 1)
                dve.wait_ge(mhi_done, b + 1)
                nc.vector.tensor_tensor(mhl[:, b, :, H:2 * H], mx[:, b], mhl[:, b, :, 0:H],
                                        ALU.subtract).then_inc(mhl_done, 1)

            def normalise(b, pair):
                key = ("av", b, pair)
                T.wait_full(dve, key)
                v = T.bank(key)[:, 0:4 * VW].rearrange("p (h e) -> p h e", e=HD + 1)
                nc.vector.reciprocal(rs[:, b, pair], v[:, :, HD]).then_inc(rs_done, 1)
                dve.wait_ge(rs_done, 2 * b + pair + 1)
                if b >= 2:
                    T.wait_full(dve, ("oT", b - 2))
                nc.vector.tensor_tensor(at0[:, b % 2, 2 * pair:2 * pair + 2].rearrange("p t (h e) -> p (t h) e", e=HD),
                                        v[:, :, 0:HD], rs[:, b, pair].unsqueeze(2).broadcast_to([P, 32, HD]),
                                        ALU.mult).then_inc(T.freed_sem(key), 1)

            def residual(l, b):
                key = ("y", l, b)
                T.wait_full(dve, key)
                src = xs
                if l < 2:
                    dve.wait_ge(bias_done, B * l + b + 1)
                    src = xb
                y = T.bank(key)[:].rearrange("p (t d) -> p t d", t=TILES)
                if l == 2:
                    dve.wait_ge(r1_done, b + 1)
                    for t in range(TILES):
                        last = nc.vector.scalar_tensor_tensor(xs[:, b, t], y[:, t], r1[:, b, t:t + 1], xs[:, b, t],
                                                              ALU.mult, ALU.add)
                else:
                    last = nc.vector.tensor_tensor(xs[:, b], y, src[:, b], ALU.add)
                last.then_inc(T.freed_sem(key), 1)

            def relu(b):
                for f in range(1, F0, 2):
                    key = ("h", b, f)
                    SR.wait_full(dve, key)
                    if b >= 2 and f == 1:
                        T.wait_full(dve, ("y", 1, b - 2))
                    nc.vector.tensor_scalar(hT[:, b % 2, f], SR.bank(key)[:], L["b1"][:, f:f + 1], 0.0, ALU.add,
                                            ALU.max).then_inc(SR.freed_sem(key), 1)

            def keys_values1():
                w = B * KV
                T.wait_full(dve, ("k1",))
                nc.vector.tensor_scalar(k1[:], T.bank(("k1",))[:, 0:w], L["bk1"], None, ALU.add)\
                    .then_inc(T.freed_sem(("k1",)), 1)
                for key, dst in ((("kq",), kq), (("bq",), bqk)):
                    T.wait_full(dve, key)
                    nc.vector.tensor_copy(dst[:], T.bank(key)[:, 0:w]).then_inc(T.freed_sem(key), 1)
                T.wait_full(dve, ("v1",))
                nc.vector.tensor_tensor(v1[:], T.bank(("v1",))[0:KV, :].rearrange("p (b d) -> p b d", b=B),
                                        R["bv1"][0:KV].unsqueeze(1).broadcast_to([KV, B, D]),
                                        ALU.add).then_inc(T.freed_sem(("v1",)), 1)

            def softmax1(b):
                key = ("sim", b)
                T.wait_full(dve, key)
                if b == 0:
                    T.wait_taken(dve, ("bq",))
                if b >= 2:
                    dve.wait_ge(p1_done, b - 1)
                s_ = sm[:, b % 2]
                nc.vector.tensor_tensor(s_, T.bank(key)[:, 0:TILES * KV].rearrange("p (t k) -> p t k", t=TILES),
                                        bqk[:, b * KV:(b + 1) * KV].unsqueeze(1).broadcast_to([P, TILES, KV]),
                                        ALU.add).then_inc(T.freed_sem(key), 1)
                T.wait_taken(dve, key)
                nc.vector.tensor_reduce(m1[:, b], s_, AX.X, ALU.max).then_inc(sim_max, 1)
                dve.wait_ge(sim_max, b + 1)
                nc.vector.tensor_tensor(s_, s_, m1[:, b].unsqueeze(2).broadcast_to([P, TILES, KV]),
                                        ALU.subtract).then_inc(sim_sub, 1)

            def sums1(b):
                dve.wait_ge(p1_done, b + 1)
                nc.vector.tensor_reduce(s1[:, b], p1[:, b % 2], AX.X, ALU.add).then_inc(s1_done, 1)
                dve.wait_ge(s1_done, b + 1)
                nc.vector.reciprocal(r1[:, b], s1[:, b]).then_inc(r1_done, 1)

            def gated(b):
                for f in range(F1):
                    key = ("up", b, f)
                    SR.wait_full(dve, key)
                    ER.wait_taken(dve, ("gate", b, f))
                    if b >= 2 and f == 0:
                        T.wait_full(dve, ("y", 3, b - 2))
                    nc.vector.scalar_tensor_tensor(hT[:, b % 2, f], SR.bank(key)[:], QSCALE * QSCALE,
                                                   sg[:, (b * F1 + f) % 3], ALU.mult, ALU.mult)\
                        .then_inc(SR.freed_sem(key), 1)

            ln_begin(0, 0)
            ln_end(0, 0)
            ln_begin(0, 1)
            q_lo(0)
            keys0()
            ln_end(0, 1)
            ln_begin(0, 2)
            q_lo(1)
            abs_sums()
            ln_end(0, 2)
            for t, g in s_units():
                maxima(0, t, g)
            max_parts(0)
            values0()
            ternary()
            ln_begin(0, 3)
            q_lo(2)
            ln_end(0, 3)
            for b in range(B):
                if b + 1 < B:
                    for t, g in s_units():
                        maxima(b + 1, t, g)
                    max_parts(b + 1)
                else:
                    keys_values1()
                if b:
                    ln_end(1, b - 1)
                if b == 3:
                    x_lo(1, 0)
                normalise(b, 0)
                normalise(b, 1)
                if b == 0:
                    q_lo(3)
                residual(0, b)
                ln_begin(1, b)
            x_lo(1, 1)
            ln_end(1, 3)
            relu(0)
            x_lo(1, 2)
            relu(1)
            residual(1, 0)
            x_lo(1, 3)
            ln_begin(2, 0)
            relu(2)
            residual(1, 1)
            relu(3)
            ln_end(2, 0)
            residual(1, 2)
            softmax1(0)
            ln_begin(2, 1)
            ln_end(2, 1)
            residual(1, 3)
            for b in range(1, B):
                ln_begin(2, b + 1) if b + 1 < B else ln_begin(3, 0)
                softmax1(b)
                sums1(b - 1)
                ln_end(2, b + 1) if b + 1 < B else ln_end(3, 0)
                residual(2, b - 1)
            x_lo(3, 0)
            sums1(3)
            gated(0)
            residual(2, 3)
            for b in range(1, B):
                ln_begin(3, b)
                ln_end(3, b)
                x_lo(3, b)
                gated(b)
                residual(3, b - 1)
            residual(3, 3)


def kernel(**inputs):
    import concourse.bacc as bacc
    from concourse.bass_utils import run_bass_kernel_spmd

    a = {k: np.asarray(v) for k, v in inputs.items()}

    def pack(widths, parts, dtype=np.float32):
        cols, n = columns(widths)
        out = np.zeros((P, n), dtype)
        for name, c in cols.items():
            v = parts[name]
            out[:v.shape[0], c] = v.reshape(v.shape[0], -1)
        return out

    ctxp = np.zeros((P, B, 3, KP), np.float32)
    ctxp[:, :, :, :KV] = a["ctx_1024"].transpose(2, 0, 1)[:, :, None, :]
    wk0T, bk0 = a["L0_xattn_Wk"].T, a["L0_xattn_bk"]
    wk0 = np.stack([np.tile(wk0T[:, 32 * g:32 * g + 32], (1, 3)) for g in range(G)], 1)
    bk0s = np.stack([np.tile(bk0[32 * g:32 * g + 32], 3) for g in range(G)], 1)
    r = np.arange(96)
    headmask = (r[:, None] % 32 // HD == np.arange(HG)).astype(np.float32)
    lorows = -(r // 32 == 1).astype(np.float32)[:, None]
    hk = np.arange(CH * P).reshape(CH, P).T
    key, head = hk % KP, hk // KP
    vmask = ((key < KV)[:, :, None] & (head[:, :, None] == 8 * (np.arange(CH) // HALF)[None, :, None]
                                       + np.arange(8))).astype(np.float32)
    q = np.arange(P)
    kcol = np.tile(np.arange(KP), HG)
    masks = np.where((kcol[None] > q[:, None]) & (kcol[None] < KV), NEG, 0).astype(np.float32)
    maskt = np.where((key[:, :, None] > np.arange(78)) & (key < KV)[:, :, None], NEG, 0).astype(np.float32)
    selector = np.zeros((2, H, 2, KC), np.float32)
    for h in range(H):
        g, j = divmod(h, HG)
        col = (g % 2) * (GK + P) + j * KP
        selector[:, h, g // 2, col:col + KV] = -1.0

    arrays = {
        "x": np.ascontiguousarray(a["x"].reshape(B * S, D)),
        "early": pack(EARLY, {"ctxp": ctxp, "wk0": wk0, "wq0": a["L0_xattn_Wq"].T, "bq0": a["L0_xattn_bq"][:, None],
                              "bk0": bk0s, "headmask": headmask, "lorows": lorows,
                              "ident": np.eye(P, dtype=np.float32)}),
        "late": pack(LATE, {"wv0": a["L0_xattn_Wv"].T, "wo0": a["L0_xattn_Wo"].T, "w1": a["L0_ffn_W1"].T,
                            "w2": a["L0_ffn_W2"].T.reshape(F0, P, D).transpose(1, 0, 2),
                            "b1": a["L0_ffn_b1"].reshape(F0, P).T,
                            "wk1": a["L1_xattn_Wk"], "wq1": a["L1_xattn_Wq"].T, "wv1": a["L1_xattn_Wv"],
                            "bk1": a["L1_xattn_bk"][:, None], "bq1": a["L1_xattn_bq"][:, None],
                            "vmask": vmask, "masks": masks, "maskt": maskt}),
        "rows": np.concatenate([a["L0_xattn_bv"], a["L0_xattn_bo"], a["L0_ffn_b2"], a["L1_xattn_bv"]]),
        "ints": pack(INTS, {"gate": a["L1_ffn_w_gate"].T, "up": a["L1_ffn_w_up"].T,
                            "down": a["L1_ffn_w_down"].T.reshape(F1, P, D).transpose(1, 0, 2)}, np.int32),
        "selector": selector.reshape(2 * H, 2 * KC),
    }
    nc = bacc.Bacc("TRN2", target_bir_lowering=False, num_devices=1)
    args = [nc.dram_tensor(f"in_{n}", v.shape, mybir.dt.from_np(v.dtype), kind="ExternalInput").ap()
            for n, v in arrays.items()]
    out = nc.dram_tensor("out", (B * S, D), F32, kind="ExternalOutput").ap()
    build(nc, *args, out)
    got = run_bass_kernel_spmd(nc, [{f"in_{n}": v for n, v in arrays.items()}], core_ids=[0])
    return got.results[0]["out"].reshape(B, S, D)
```

```python
from contextlib import ExitStack

import numpy as np

import concourse.bass as bass
from concourse import mybir

F32 = mybir.dt.float32
F32R = mybir.dt.float32r
BF16 = mybir.dt.bfloat16
I32 = mybir.dt.int32
ALU = mybir.AluOpType
ACT = mybir.ActivationFunctionType
AX = mybir.AxisListType

P = 128
B, S, D = 4, 512, 128
TILES = S // P
KV = 77
H, HD = 16, 8
KP = 80
G = 4
HG = H // G
GK = HG * KP
CH = H * KP // P
HALF = CH // 2
V_CHUNKS = (range(0, 3), range(3, HALF))
GROUP_FROM = {0: 0, 2: 1, HALF: 2, HALF + 2: 3}
WARM = 15
ACT_TILES = 3
QSLOTS = 3
KC = 2 * GK + P
VW = 2 * HG * (HD + 1)
F0 = 512 // P
F1 = 384 // P
EPS = 1e-5
NEG = -1e30
QSCALE = 1.0 / 127.0

FIRST = {"ident": P, "wq0x3": G * 96, "bq0x3": G, "wq0": P, "bq0": 1}
EARLY = {"wk0": G * 96, "bk0": G, "headmask": HG, "ctxp": B * 240}
LATE = {"wv0": P, "bv0": 1, "wo0": P, "w1": 512, "w2": 512, "b1": F0, "wk1": P, "wq1": P, "wv1": P,
        "bk1": 1, "bq1": 1, "vmask": CH * 8}
MASKS = {"ident16": P, "masks": GK, "maskt": CH * 78}
ROWS = {"bo0": P, "b2": P, "bv1": P}
INTS = {"gate": 384, "up": 384, "down": 384}


def columns(widths):
    at, out = 0, {}
    for name, w in widths.items():
        out[name] = slice(at, at + w)
        at += w
    return out, at


class Ring:

    def __init__(self, banks, full, freed, keys):
        self.banks, self.full, self.freed = banks, full, freed
        self.at = {k: n for n, k in enumerate(keys)}
        assert len(self.at) == len(keys)

    def bank(self, key):
        return self.banks[self.at[key] % len(self.banks)]

    def full_sem(self, key):
        return self.full[self.at[key] % len(self.banks)]

    def freed_sem(self, key):
        return self.freed[self.at[key] % len(self.banks)]

    def claim(self, eng, key):
        n = self.at[key] // len(self.banks)
        if n:
            eng.wait_ge(self.freed_sem(key), n)

    def wait_full(self, eng, key):
        eng.wait_ge(self.full_sem(key), self.at[key] // len(self.banks) + 1)

    def wait_taken(self, eng, key):
        eng.wait_ge(self.freed_sem(key), self.at[key] // len(self.banks) + 1)


def tensor_steps():
    u = [("s", 0, t, g) for t, g in s_units()]
    s = [("xT", 0, 0), ("k0",), ("q0",)] + u[:5] + [("xT", 0, 1)] + u[5:8] + [("q", 1)] + u[8:]
    s += [("xT", 0, 2), ("m", 0)]
    s += mix(0)
    s += mix(1)
    s += mix(2)
    s += mix(3)
    a = av_units(3)
    s += [("oT", 2)] + a[:2] + [("y", 0, 2)] + a[2:5] + [("xT", 1, 0)] + a[5:]
    s += [("h", 0), ("oT", 3), ("xT", 1, 1), ("y", 0, 3), ("y", 1, 0), ("xT", 1, 2), ("h", 1), ("xT", 1, 3),
          ("h", 2), ("y", 1, 1), ("xT", 2, 0), ("sim", 0), ("h", 3), ("y", 1, 2), ("xT", 2, 1), ("pT", 0),
          ("y", 1, 3), ("sim", 1), ("y", 2, 0), ("xT", 2, 2), ("sim", 2), ("pT", 1), ("xT", 2, 3), ("y", 2, 1),
          ("sim", 3), ("pT", 2), ("y", 2, 2), ("xT", 3, 0), ("pT", 3), ("xT", 3, 1), ("gu", 0), ("y", 2, 3),
          ("gu", 1), ("xT", 3, 2), ("y", 3, 0), ("gu", 2), ("xT", 3, 3), ("y", 3, 1), ("gu", 3), ("y", 3, 2),
          ("y", 3, 3)]
    return s


def norm_order():
    return [(0, b) for b in range(B)] + [(1, 0), (1, 1), (1, 2), (1, 3), (2, 0), (2, 1), (2, 2), (2, 3),
                                         (3, 0), (3, 1), (3, 2), (3, 3)]


def av_units(b):
    return [("av", b, t, u) for t in range(TILES) for u in range(2)]


def mix(b):
    p = [("p", b, c) for c in range(CH)]
    s = [("s", b + 1, t, g) for t, g in s_units()] if b + 1 < B else []
    a = av_units(b - 1) if b else [("v0", vb, u) for vb in range(B) for u in range(2)]

    def some(queue, n):
        out = queue[:n]
        del queue[:n]
        return out

    def only(there, *steps):
        return list(steps) if there else []

    if b == 0:
        out = some(a, 1) + some(p, 3) + some(a, 3) + [("q", 2)]
        for n in (3, 3, 3, 3, 3):
            out += some(s, n) + some(p, 1)
        return out + s + some(a, 1) + some(p, 1) + [("m", 1)] + some(a, 1) + some(p, 1) + a + p
    out = some(p, 2) + only(b >= 2, ("oT", b - 2)) + only(b == 1, ("xT", 0, 3))
    out += some(a, 1) + only(b == 3, ("gamma",)) + some(p, 1) + some(s, 3)
    out += some(a, 1) + only(b == 1, ("q", 3)) + only(b >= 2, ("y", 0, b - 2)) + some(p, 1) + some(s, 3)
    out += some(a, 1) + only(b == 3, ("k1",)) + some(p, 1) + some(s, 3)
    out += some(a, 1) + some(p, 1) + some(s, 3) + some(p, 1) + some(s, 2)
    out += some(a, 1) + some(p, 1) + some(s, 2) + some(a, 1) + some(p, 1)
    out += only(b + 1 < B, ("m", b + 1)) + some(a, 1) + some(p, 1) + a
    out += only(b == 3, ("kq",), ("bq",), ("v1",))
    return out


def s_units():
    return [(t, g) for t in range(TILES) for g in range(G)]


def ring_keys(steps):
    t, s, e = [], [], []
    for st in steps:
        k = st[0]
        if k == "av":
            if st[2] % 2 == 0 and st[3] == 0:
                t.append(("av", st[1], st[2] // 2))
        elif k == "xT" and st[1] in (0, 2) or k in ("pT", "q"):
            e.append(st)
        elif k in ("sim", "s", "v0", "gamma", "k1", "kq", "bq", "v1"):
            s.append(st)
        elif k in ("k0", "q0"):
            e += [(k, g) for g in range(G)]
        elif k == "p":
            e.append(st)
        elif k == "h":
            e += [("h", st[1], f) for f in range(0, F0, 2)]
            s += [("h", st[1], f) for f in range(1, F0, 2)]
        elif k == "gu":
            e += [("gate", st[1], f) for f in range(F1)]
            s += [("up", st[1], f) for f in range(F1)]
        else:
            t.append(st)
    return t, s, e


def build(nc, x, first, early, masks, late, rows, ints, selector, out):
    fc, fn = columns(FIRST)
    ec, en = columns(EARLY)
    lc, ln_ = columns(LATE)
    mc, mn = columns(MASKS)
    rc, rn = columns(ROWS)
    ic, inn = columns(INTS)
    steps = tensor_steps()
    x_dram = x.rearrange("(b t p) d -> b p t d", b=B, p=P)
    out_dram = out.rearrange("(b t p) d -> b p t d", b=B, p=P)

    with ExitStack() as ctx:
        def sb(name, shape, dt=F32):
            return ctx.enter_context(nc.sbuf_tensor(name, shape, dt))

        def sem(name):
            return ctx.enter_context(nc.semaphore(name))

        def ring(name, n, keys):
            banks = [ctx.enter_context(nc.psum_tensor(f"{name}{i}", [P, 512], F32)) for i in range(n)]
            full, freed = ([sem(f"{name}_{what}{i}") for i in range(n)] for what in ("full", "freed"))
            return Ring(banks, full, freed, keys)

        tk, sk, ek = ring_keys(steps)
        T = ring("turn", 2, tk)
        SR = ring("score", 3, sk)
        ER = ring("exp", 3, ek)

        fw = sb("first_sb", [P, fn])
        ew = sb("early_sb", [P, en])
        lw = sb("late_sb", [P, ln_])
        rw = sb("rows_sb", [P, rn])
        iw = sb("ints_sb", [P, inn], I32)
        E = {n: fw[:, c] for n, c in fc.items()} | {n: ew[:, c] for n, c in ec.items()}
        L = {n: lw[:, c] for n, c in lc.items()}
        R = {n: rw[:, c] for n, c in rc.items()}
        mw = sb("masks_sb", [P, mn], BF16)
        ident16, masks16, maskt16 = (mw[:, mc[n]] for n in ("ident16", "masks", "maskt"))
        ctxp = E["ctxp"].rearrange("p (b c) -> p b c", b=B)
        ident = E["ident"]
        w1q = sb("w1_ternary", [P, 512], F32R)
        w2q = sb("w2_ternary", [P, 512])
        gu_w = sb("gate_up_w", [P, 768], F32R)
        down_w = sb("down_w", [P, 384])
        ones = sb("ones", [P, P])
        silu_of_one = sb("silu_of_one", [1, 1])
        half = sb("minus_half", [P, TILES])
        gsum = sb("abs_sums", [P, 2])
        thr = sb("threshold", [P, 4])
        kst = sb("k0_stack", [P, B, 2, KC], F32R)
        below = sb("below", [P, 512])
        vx = sb("v0_block", [P, B, CH, VW])
        k1 = sb("k1T", [P, B * KV])
        kq = sb("wq_k1", [P, B * KV])
        bqb = sb("bq1_columns", [P, P])
        bqk = sb("bq1_k1", [P, B * KV])
        v1 = sb("v1", [KV, B, D])
        xs = sb("x_sb", [P, B, TILES, D])
        xb = sb("x_bias", [P, B, TILES, D])
        xh = sb("x_hat", [P, B, TILES, D])
        xt = sb("x_hatT", [P, B, S])
        hi = sb("hi", [P, B, S], F32R)
        lo = sb("lo", [P, B, S], F32R)
        stats = sb("bn_stats", [P, B, TILES, 6])
        mv = sb("mean_var", [P, B, TILES, 2])
        ve = sb("var_eps", [P, B, TILES])
        rstd = sb("rstd", [P, B, TILES])
        qst = sb("q_stack", [P, QSLOTS, G, S], F32R)
        mx = sb("max0", [P, B, TILES, H])
        mhl = sb("max0_hi_lo", [P, TILES, P])
        nmean = sb("minus_mean", [P, B, TILES])
        shift = sb("minus_mean_rstd", [P, B, TILES])
        pr = sb("probs0", [P, 2, CH, S])
        rs = sb("rsum0", [P, B, 2, 32])
        at0 = sb("attn0", [P, 2, TILES, D])
        at0T = sb("attn0T", [P, 2, S])
        m1 = sb("max1", [P, B, TILES])
        s1 = sb("sum1", [P, B, TILES])
        r1 = sb("rsum1", [P, B, TILES])
        khi = pr[0:96, 1, 0:3].rearrange("p c q -> p (c q)")[:, 0:G * B * KV].bitcast(F32R)
        hT = pr[:, :, 0:F0]
        sg = pr[:, 0, F0:F0 + 3]
        p1T = pr[0:KV, :, F0 + 3]
        sm = pr[:, :, F0 + 4, 0:TILES * KV].rearrange("p s (t k) -> p s t k", t=TILES)
        p1 = pr[:, :, F0 + 5, 0:TILES * KV].rearrange("p s (t k) -> p s t k", t=TILES)

        first_in, masks_in = sem("first_in"), sem("masks_in")
        early_in, late_in, rows_in, ints_in = sem("early_in"), sem("late_in"), sem("rows_in"), sem("ints_in")
        x_in = [sem(f"x_in{b}") for b in range(B)]
        sel_in = sem("selector_in")
        q_in = [sem(f"q_stack_in{b}") for b in range(B)]
        out_done = sem("out_done")
        ln_stats, ln_mv, ln_ve, ln_rstd, ln_shift, ln_xh, ln_xh_pool = (
            sem(n) for n in ("ln_stats", "ln_mv", "ln_ve", "ln_rstd", "ln_shift", "ln_xhat", "ln_xhat_pool"))
        hi_done = sem("hi_done")
        bias_done = sem("bias_done")
        consts = sem("consts_done")
        kzero = sem("k_stack_zeroed")
        dprep = sem("vector_prep")
        khi_done = sem("k_hi_done")
        kfirst = sem("k_first_batch")
        krest = sem("k_other_batches")
        q0hi_done = sem("q0_hi_done")
        vones = sem("v_ones_done")
        mzero = sem("max_columns_zeroed")
        mrow_part = sem("max_rows_part")
        wq_done = sem("ternary_done")
        i_done = sem("int_weights_done")
        bq_done = sem("bq_columns_done")
        mhi_done, mhl_done = sem("max_hi_done"), sem("max_hi_lo_done")
        rs_done = sem("rsum0_done")
        sim_max, p1_done, s1_done, r1_done = (
            sem(n) for n in ("sim_max", "probs1_done", "sum1_done", "rsum1_done"))
        half_done = sem("minus_half_done")

        block = ctx.enter_context(nc.Block())

        hi_order = [("q", b) for b in range(1, B)] + [("x", 1, b) for b in range(B)] + [("x", 3, b) for b in range(B)]
        norm_at = {k: n for n, k in enumerate(norm_order())}
        hi_at = {k: n + 1 for n, k in enumerate(hi_order)}

        @block.sync
        def _(sp):
            sp.dma_start(xs[:, 0], x_dram[0]).then_inc(x_in[0], 16)
            sp.dma_start(fw[:], first).then_inc(first_in, 16)
            sp.dma_start(ew[:], early).then_inc(early_in, 16)
            sp.dma_start(xs[:, 1], x_dram[1]).then_inc(x_in[1], 16)
            sp.dma_start(xs[:, 2], x_dram[2]).then_inc(x_in[2], 16)
            sp.dma_start(mw[:], masks).then_inc(masks_in, 16)
            sp.dma_start(lw[:], late).then_inc(late_in, 16)
            sp.dma_start(rw[:], rows.partition_broadcast(P)).then_inc(rows_in, 16)
            sp.dma_start(xs[:, 3], x_dram[3]).then_inc(x_in[3], 16)

            for b in range(1, B):
                if b >= QSLOTS:
                    ER.wait_taken(sp, ("p", b - QSLOTS, CH - 1))
                sp.wait_ge(hi_done, hi_at["q", b])
                for part in range(2):
                    for g in range(G):
                        sp.dma_start(qst[32 * part:32 * part + 32, b % QSLOTS, g].bitcast(F32),
                                     hi[32 * g:32 * g + 32, b].bitcast(F32)).then_inc(q_in[b], 16)
                ER.wait_taken(sp, ("q", b))
                for g in range(G):
                    sp.dma_start(qst[64:96, b % QSLOTS, g].bitcast(F32),
                                 lo[32 * g:32 * g + 32, b].bitcast(F32)).then_inc(q_in[b], 16)
                if b == 1:
                    sp.dma_start(iw[:], ints).then_inc(ints_in, 16)
            for b in range(B):
                T.wait_taken(sp, ("y", 3, b))
                sp.dma_start(out_dram[b], xs[:, b]).then_inc(out_done, 16)
            sp.wait_ge(out_done, 16 * B)

        @block.tensor
        def _(pe):
            def turn_x(l, b):
                key = ("xT", l, b)
                ring_ = ER if l in (0, 2) else T
                ring_.claim(pe, key)
                if l == 0 and b == 0:
                    pe.wait_ge(first_in, 16)
                pe.wait_ge(ln_xh, norm_at[l, b] + 1)
                pe.wait_ge(ln_xh_pool, norm_at[l, b] + 1)
                for t in range(TILES):
                    last = nc.tensor.transpose(ring_.bank(key)[:, t * P:(t + 1) * P], xh[:, b, t], ident)
                last.then_inc(ring_.full_sem(key), 1)

            def project_q(b):
                ER.claim(pe, ("q", b))
                ER.wait_taken(pe, ("xT", 0, b))
                nc.tensor.matmul(ER.bank(("q", b))[:], E["wq0"], xt[:, b], start=True,
                                 stop=True).then_inc(ER.full_sem(("q", b)), 1)

            def keys0():
                pe.wait_ge(early_in, 16)
                for g in range(G):
                    ER.claim(pe, ("k0", g))
                    nc.tensor.matmul(ER.bank(("k0", g))[0:96, 0:B * KV].rearrange("p (b k) -> p b k", b=B),
                                     E["wk0"][:, g * 96:(g + 1) * 96], ctxp[:, :, 0:KV],
                                     start=True, stop=True).then_inc(ER.full_sem(("k0", g)), 1)

            def queries0():
                ER.wait_taken(pe, ("xT", 0, 0))
                for g in range(G):
                    ER.claim(pe, ("q0", g))
                    nc.tensor.matmul(ER.bank(("q0", g))[0:96, :], E["wq0x3"][:, g * 96:(g + 1) * 96], xt[:, 0],
                                     start=True, stop=True).then_inc(ER.full_sem(("q0", g)), 1)

            def values0(b, u):
                key = ("v0", b, u)
                SR.claim(pe, key)
                if b == 0 and u == 0:
                    pe.wait_ge(late_in, 16)
                for n, c in enumerate(V_CHUNKS[u]):
                    off = (P * c) % KP
                    last = nc.tensor.matmul(SR.bank(key)[:, P * n:P * (n + 1)], ctxp[:, b, off:off + P],
                                            L["wv0"], start=True, stop=True)
                last.then_inc(SR.full_sem(key), 1)

            def gamma():
                SR.claim(pe, ("gamma",))
                pe.wait_ge(consts, 1)
                pe.wait_ge(dprep, 2)
                nc.tensor.matmul(SR.bank(("gamma",))[:, 0:2], ones[:], gsum[:], start=True,
                                 stop=True).then_inc(SR.full_sem(("gamma",)), 1)

            def scores(b, t, g):
                key = ("s", b, t, g)
                if (t, g) == (0, 0):
                    if b:
                        pe.wait_ge(q_in[b], 16 * 3 * G)
                    if b == 0:
                        for g0 in range(1, G):
                            ER.wait_taken(pe, ("q0", g0))
                        pe.wait_ge(kzero, 2)
                        pe.wait_ge(kfirst, 3)
                        pe.wait_ge(masks_in, 16)
                    if b == 1:
                        pe.wait_ge(krest, 3)
                SR.claim(pe, key)
                o = SR.bank(key)[:, 0:GK]
                kcol = (g % 2) * (GK + P)
                last = nc.tensor.matmul(o, qst[0:96, b % QSLOTS, g, t * P:(t + 1) * P],
                                        kst[0:96, b, g // 2, kcol:kcol + GK], start=True, stop=t > 0)
                if t == 0:
                    last = nc.tensor.matmul(o, ident16, masks16, start=False, stop=True)
                last.then_inc(SR.full_sem(key), 1)

            def scores_t(b, c):
                key = ("p", b, c)
                if b == 0 and c == 0:
                    pe.wait_ge(sel_in, 16)
                if c in GROUP_FROM:
                    g = GROUP_FROM[c]
                    if g < G - 1:
                        pe.wait_ge(mrow_part, (G - 1) * b + g + 1)
                    else:
                        T.wait_taken(pe, ("m", b))
                ER.claim(pe, key)
                o = ER.bank(key)[:]
                u, i = divmod(c, HALF)
                parts = {0: [(0, 0)], 1: [(P, 0)], 2: [(2 * P, 0), (3 * P, 1)], 3: [(4 * P, 1)], 4: [(5 * P, 1)]}[i]
                for n, (col, g) in enumerate(parts):
                    nc.tensor.matmul(o, kst[:, b, u, col:col + P], qst[:, b % QSLOTS, 2 * u + g],
                                     start=n == 0, stop=n == len(parts) - 1)
                nc.tensor.matmul(o[:, 0:78], ident16, maskt16[:, 78 * c:78 * c + 78],
                                 start=False, stop=True, skip_group_check=True).then_inc(ER.full_sem(key), 1)

            def turn_max(b):
                key = ("m", b)
                T.claim(pe, key)
                pe.wait_ge(mhl_done, b + 1)
                for t in range(TILES):
                    last = nc.tensor.transpose(T.bank(key)[:, t * P:(t + 1) * P], mhl[:, t], ident)
                last.then_inc(T.full_sem(key), 1)

            def attend(b, t, u):
                key = ("av", b, t // 2)
                if (t % 2, u) == (0, 0):
                    T.claim(pe, key)
                if (t, u) == (0, 0):
                    for c in range(CH - 3, CH):
                        ER.wait_taken(pe, ("p", b, c))
                    if b == 0:
                        for vb, vu in ((2, 1), (3, 0), (3, 1)):
                            SR.wait_taken(pe, ("v0", vb, vu))
                        pe.wait_ge(vones, 1)
                n = (t % 2) * 2 + u
                for c in range(HALF):
                    last = nc.tensor.matmul(T.bank(key)[:, n * VW:(n + 1) * VW],
                                            pr[:, b % 2, u * HALF + c, t * P:(t + 1) * P], vx[:, b, u * HALF + c],
                                            start=n == 0 and c == 0, stop=n == 3 and c == HALF - 1,
                                            skip_group_check=True)
                if n == 3:
                    last.then_inc(T.full_sem(key), 1)

            def turn_attended(b):
                key = ("oT", b)
                T.claim(pe, key)
                for pair in range(2):
                    T.wait_taken(pe, ("av", b, pair))
                for t in range(TILES):
                    last = nc.tensor.transpose(T.bank(key)[:, t * P:(t + 1) * P], at0[:, b % 2, t], ident)
                last.then_inc(T.full_sem(key), 1)

            def output(l, b, lhs, rhs):
                key = ("y", l, b)
                T.claim(pe, key)
                n = len(rhs)
                for t in range(TILES):
                    for f in range(n):
                        last = nc.tensor.matmul(T.bank(key)[:, t * P:(t + 1) * P], lhs(f, t), rhs[f],
                                                start=f == 0, stop=f == n - 1)
                last.then_inc(T.full_sem(key), 1)

            def hidden0(b):
                T.wait_taken(pe, ("xT", 1, b))
                if b == 0:
                    pe.wait_ge(wq_done, 2)
                for f in range(F0):
                    ring_ = SR if f % 2 else ER
                    key = ("h", b, f)
                    ring_.claim(pe, key)
                    nc.tensor.matmul(ring_.bank(key)[:], w1q[:, f * P:(f + 1) * P], hi[:, b], start=True, stop=False)
                    nc.tensor.matmul(ring_.bank(key)[:], w1q[:, f * P:(f + 1) * P], lo[:, b],
                                     start=False, stop=True).then_inc(ring_.full_sem(key), 1)

            def keys1():
                SR.claim(pe, ("k1",))
                nc.tensor.matmul(SR.bank(("k1",))[:, 0:B * KV].rearrange("p (b k) -> p b k", b=B), L["wk1"],
                                 ctxp[:, :, 0:KV], start=True, stop=True).then_inc(SR.full_sem(("k1",)), 1)

            def project_keys1(key, weights):
                SR.claim(pe, key)
                SR.wait_taken(pe, ("k1",))
                nc.tensor.matmul(SR.bank(key)[:, 0:B * KV], weights, k1[:], start=True, stop=True)\
                    .then_inc(SR.full_sem(key), 1)

            def values1():
                SR.claim(pe, ("v1",))
                for b in range(B):
                    last = nc.tensor.matmul(SR.bank(("v1",))[0:KV, b * D:(b + 1) * D], ctxp[:, b, 0:KV], L["wv1"],
                                            start=True, stop=True)
                last.then_inc(SR.full_sem(("v1",)), 1)

            def sim1(b):
                key = ("sim", b)
                SR.claim(pe, key)
                if b == 0:
                    SR.wait_taken(pe, ("bq",))
                o = SR.bank(key)[:, 0:TILES * KV].rearrange("p (t k) -> p t k", t=TILES)
                bq_row = bqk[0:1, b * KV:(b + 1) * KV].unsqueeze(1).broadcast_to([1, TILES, KV])
                nc.tensor.matmul(o, ones[0:1, :], bq_row, start=True, stop=True)
                ER.wait_taken(pe, ("xT", 2, b))
                for t in range(TILES):
                    last = nc.tensor.matmul(o[:, t], xt[:, b, t * P:(t + 1) * P], kq[:, b * KV:(b + 1) * KV],
                                            start=False, stop=True, skip_group_check=True)
                last.then_inc(SR.full_sem(key), 1)

            def turn_probs1(b):
                key = ("pT", b)
                ER.claim(pe, key)
                pe.wait_ge(p1_done, b + 1)
                for t in range(TILES):
                    last = nc.tensor.transpose(ER.bank(key)[0:KV, t * P:(t + 1) * P], p1[:, b % 2, t], ident)
                last.then_inc(ER.full_sem(key), 1)

            def gate_up(b):
                T.wait_taken(pe, ("xT", 3, b))
                if b == 0:
                    pe.wait_ge(i_done, 3)
                for f in range(F1):
                    for ring_, key, col in ((ER, ("gate", b, f), 0), (SR, ("up", b, f), 384)):
                        ring_.claim(pe, key)
                        w = gu_w[:, col + f * P:col + (f + 1) * P]
                        nc.tensor.matmul(ring_.bank(key)[:], w, hi[:, b], start=True, stop=False)
                        nc.tensor.matmul(ring_.bank(key)[:], w, lo[:, b], start=False,
                                         stop=True).then_inc(ring_.full_sem(key), 1)

            pe.wait_ge(consts, 1)
            for _ in range(WARM):
                nc.tensor.matmul(T.banks[0][:, 0:P], ones[:], ones[:], start=True, stop=True)
            for st in steps:
                k, *n = st
                b = n[-1] if n else 0
                if k == "xT":
                    turn_x(*n)
                elif k == "q":
                    project_q(b)
                elif k == "q0":
                    queries0()
                elif k == "k0":
                    keys0()
                elif k == "v0":
                    values0(*n)
                elif k == "gamma":
                    gamma()
                elif k == "s":
                    scores(*n)
                elif k == "m":
                    turn_max(b)
                elif k == "p":
                    scores_t(*n)
                elif k == "av":
                    attend(*n)
                elif k == "oT":
                    turn_attended(b)
                elif k == "k1":
                    keys1()
                elif k == "kq":
                    project_keys1(("kq",), L["wq1"])
                elif k == "bq":
                    pe.wait_ge(bq_done, 1)
                    project_keys1(("bq",), bqb[:])
                elif k == "v1":
                    values1()
                elif k == "h":
                    hidden0(b)
                elif k == "sim":
                    sim1(b)
                elif k == "pT":
                    turn_probs1(b)
                elif k == "gu":
                    gate_up(b)
                elif st[:2] == ("y", 0):
                    T.wait_taken(pe, ("oT", b))
                    output(0, b, lambda f, t: at0T[:, b % 2, t * P:(t + 1) * P], [L["wo0"]])
                elif st[:2] == ("y", 1):
                    for f in range(F0):
                        (SR if f % 2 else ER).wait_taken(pe, ("h", b, f))
                    output(1, b, lambda f, t: hT[:, b % 2, f, t * P:(t + 1) * P],
                           [w2q[:, f * P:(f + 1) * P] for f in range(F0)])
                elif st[:2] == ("y", 2):
                    ER.wait_taken(pe, ("pT", b))
                    if b == 0:
                        SR.wait_taken(pe, ("v1",))
                    output(2, b, lambda f, t: p1T[:, b % 2, t * P:(t + 1) * P], [v1[:, b]])
                elif st[:2] == ("y", 3):
                    for f in range(F1):
                        SR.wait_taken(pe, ("up", b, f))
                    output(3, b, lambda f, t: hT[:, b % 2, f, t * P:(t + 1) * P],
                           [down_w[:, f * P:(f + 1) * P] for f in range(F1)])

        @block.scalar
        def _(act):
            def x_hat(l, b):
                act.wait_ge(ln_shift, norm_at[l, b] + 1)
                for t in range(ACT_TILES):
                    last = nc.scalar.activation(xh[:, b, t], xs[:, b, t], ACT.Identity, bias=shift[:, b, t:t + 1],
                                                scale=rstd[:, b, t:t + 1])
                last.then_inc(ln_xh, 1)

            def x_hi(l, b):
                T.wait_full(act, ("xT", l, b))
                nc.scalar.activation(hi[:, b], T.bank(("xT", l, b))[:], ACT.Copy).then_inc(hi_done, 1)

            def copy_xT(l, b):
                key = ("xT", l, b)
                ring_ = ER if l in (0, 2) else T
                ring_.wait_full(act, key)
                nc.scalar.activation(xt[:, b], ring_.bank(key)[:], ACT.Copy).then_inc(ring_.freed_sem(key), 1)

            def q_hi(b):
                ER.wait_full(act, ("q", b))
                nc.scalar.activation(hi[:, b], ER.bank(("q", b))[:], ACT.Identity, bias=E["bq0"]).then_inc(hi_done, 1)

            def take_max(b):
                key = ("m", b)
                T.wait_full(act, key)
                for g in range(G):
                    last = nc.scalar.activation(qst[96:P, b % QSLOTS, g], T.bank(key)[96:P, :], ACT.Copy)
                    last.then_inc(*((T.freed_sem(key), 1) if g == G - 1 else (mrow_part, 1)))

            def copy_oT(b):
                key = ("oT", b)
                T.wait_full(act, key)
                nc.scalar.activation(at0T[:, b % 2], T.bank(key)[:], ACT.Identity,
                                     bias=L["bv0"]).then_inc(T.freed_sem(key), 1)

            def keys_hi():
                act.wait_ge(early_in, 16)
                w = B * KV
                for g in range(G):
                    key = ("k0", g)
                    ER.wait_full(act, key)
                    nc.scalar.activation(khi[:, g * w:(g + 1) * w], ER.bank(key)[0:96, 0:w], ACT.Identity,
                                         bias=E["bk0"][0:96, g:g + 1]).then_inc(khi_done, 1)

            def queries0_hi(groups):
                for g in groups:
                    ER.wait_full(act, ("q0", g))
                    nc.scalar.activation(qst[0:96, 0, g], ER.bank(("q0", g))[0:96, :], ACT.Identity,
                                         bias=E["bq0x3"][0:96, g:g + 1]).then_inc(q0hi_done, 1)

            def place_keys(groups, batches, done):
                for g in groups:
                    ER.wait_taken(act, ("k0", g))
                    src = khi[:, g * B * KV:(g + 1) * B * KV].rearrange("p (b k) -> p b k", b=B)
                    for j in range(HG):
                        col = (g % 2) * (GK + P) + j * KP
                        last = nc.scalar.activation(kst[0:96, batches, g // 2, col:col + KV], src[:, batches],
                                                    ACT.Copy, scale=E["headmask"][0:96, j:j + 1])
                last.then_inc(done, 1)

            def exp(b, c):
                key = ("p", b, c)
                ER.wait_full(act, key)
                if b >= 2 and c == 0:
                    T.wait_full(act, ("av", b - 2, 1))
                nc.scalar.activation(pr[:, b % 2, c], ER.bank(key)[:], ACT.Exp,
                                     scale=HD ** -0.5).then_inc(ER.freed_sem(key), 1)

            def relu(b):
                for f in range(0, F0, 2):
                    key = ("h", b, f)
                    ER.wait_full(act, key)
                    if b >= 2 and f == 0:
                        T.wait_full(act, ("y", 1, b - 2))
                    if b == 1 and f == 0:
                        T.wait_full(act, ("av", 3, 1))
                    nc.scalar.activation(hT[:, b % 2, f], ER.bank(key)[:], ACT.Relu,
                                         bias=L["b1"][:, f:f + 1]).then_inc(ER.freed_sem(key), 1)

            def exp1(b):
                SR.wait_taken(act, ("sim", b))
                if b >= 2:
                    ER.wait_full(act, ("pT", b - 2))
                    act.wait_ge(s1_done, b - 1)
                nc.scalar.activation(p1[:, b % 2], sm[:, b % 2], ACT.Exp, scale=D ** -0.5).then_inc(p1_done, 1)

            def silu_table():
                nc.scalar.activation(silu_of_one[:], ones[0:1, 0:1], ACT.Silu)

            def silu(b):
                for f in range(F1):
                    key = ("gate", b, f)
                    ER.wait_full(act, key)
                    n = b * F1 + f
                    if n >= 3:
                        SR.wait_taken(act, ("up", *divmod(n - 3, F1)))
                    nc.scalar.activation(sg[:, n % 3], ER.bank(key)[:], ACT.Silu,
                                         scale=QSCALE).then_inc(ER.freed_sem(key), 1)

            def copy_pT(b):
                key = ("pT", b)
                ER.wait_full(act, key)
                if b >= 2:
                    T.wait_full(act, ("y", 2, b - 2))
                nc.scalar.activation(p1T[:, b % 2], ER.bank(key)[0:KV, :], ACT.Copy).then_inc(ER.freed_sem(key), 1)

            x_hat(0, 0)
            copy_xT(0, 0)
            keys_hi()
            queries0_hi(range(0, 2))
            place_keys([3], slice(0, 1), kfirst)
            queries0_hi(range(2, G))
            x_hat(0, 1)
            copy_xT(0, 1)
            q_hi(1)
            x_hat(0, 2)
            place_keys([2, 3], slice(1, B), krest)
            copy_xT(0, 2)
            take_max(0)
            act.wait_ge(late_in, 16)
            for b in range(B):
                for k, *n in mix(b):
                    if k == "p":
                        exp(*n)
                    elif k == "xT":
                        copy_xT(*n)
                    elif k == "q":
                        q_hi(*n)
                    elif k == "m":
                        take_max(*n)
                    elif k == "oT":
                        copy_oT(*n)
                    if k == "p" and n[1] == 7:
                        if b == 0:
                            x_hat(0, 3)
                        elif b >= 2:
                            x_hat(1, b - 2)
            copy_oT(2)
            x_hi(1, 0)
            x_hat(1, 2)
            relu(0)
            copy_oT(3)
            x_hi(1, 1)
            x_hat(1, 3)
            x_hi(1, 2)
            relu(1)
            x_hi(1, 3)
            relu(2)
            x_hat(2, 0)
            copy_xT(2, 0)
            x_hat(2, 1)
            exp1(0)
            relu(3)
            copy_xT(2, 1)
            copy_pT(0)
            x_hat(2, 2)
            copy_xT(2, 2)
            exp1(1)
            x_hat(2, 3)
            copy_pT(1)
            copy_xT(2, 3)
            exp1(2)
            copy_pT(2)
            x_hat(3, 0)
            exp1(3)
            x_hi(3, 0)
            x_hat(3, 1)
            copy_pT(3)
            silu_table()
            x_hi(3, 1)
            silu(0)
            x_hat(3, 2)
            silu(1)
            x_hi(3, 2)
            x_hat(3, 3)
            silu(2)
            x_hi(3, 3)
            silu(3)

        @block.gpsimd
        def _(pool):
            nc.gpsimd.memset(ones[:], 1.0).then_inc(consts, 1)
            nc.gpsimd.memset(half[:], -0.5).then_inc(half_done, 1)
            nc.gpsimd.memset(kst[0:96, :, :, GK:GK + P].bitcast(F32), 0.0).then_inc(kzero, 1)
            pads = [kst[0:96, :, :, c:c + GK].bitcast(F32).rearrange("p b u (j k) -> p b u j k", k=KP)[..., KV:KP]
                    for c in (0, GK + P)]
            for b in range(B):
                for pad in pads:
                    last = nc.gpsimd.memset(pad[:, b], 0.0)
            last.then_inc(kzero, 1)

            def rstd_of(l, b):
                n = norm_at[l, b]
                pool.wait_ge(ln_mv, n + 1)
                nc.gpsimd.tensor_scalar(ve[:, b], mv[:, b, :, 1], EPS, None, ALU.add).then_inc(ln_ve, 1)
                nc.gpsimd.tensor_scalar(nmean[:, b], mv[:, b, :, 0], -1.0, None, ALU.mult)
                pool.wait_ge(ln_ve, n + 1)
                nc.gpsimd.tensor_tensor(rstd[:, b], ve[:, b], half[:], ALU.pow).then_inc(ln_rstd, 1)
                pool.wait_ge(ln_rstd, n + 1)
                nc.gpsimd.tensor_tensor(shift[:, b], nmean[:, b], rstd[:, b], ALU.mult).then_inc(ln_shift, 1)
                for t in range(ACT_TILES, TILES):
                    last = nc.gpsimd.tensor_scalar(xh[:, b, t], xs[:, b, t], mv[:, b, t, 0:1], rstd[:, b, t:t + 1],
                                                   ALU.subtract, ALU.mult)
                last.then_inc(ln_xh_pool, 1)

            def add_bias(l, b):
                if l == 0:
                    pool.wait_ge(x_in[b], 16)
                    pool.wait_ge(rows_in, 16)
                else:
                    T.wait_taken(pool, ("y", l - 1, b))
                bias = R["bo0"] if l == 0 else R["b2"]
                nc.gpsimd.tensor_tensor(xb[:, b], xs[:, b], bias.unsqueeze(1).broadcast_to([P, TILES, D]),
                                        ALU.add).then_inc(bias_done, 1)

            def place_keys(g, batches, done):
                ER.wait_taken(pool, ("k0", g))
                src = khi[:, g * B * KV:(g + 1) * B * KV].rearrange("p (b k) -> p b k", b=B)[:, batches]
                for j in range(HG):
                    col = (g % 2) * (GK + P) + j * KP
                    last = nc.gpsimd.tensor_scalar(kst[0:96, batches, g // 2, col:col + KV], src.bitcast(F32),
                                                   E["headmask"][0:96, j:j + 1], None, ALU.mult)
                last.then_inc(done, 1)

            pool.wait_ge(half_done, 1)
            rstd_of(0, 0)
            pool.dma_start(kst[96:P].rearrange("p b u c -> p b (u c)"),
                           selector.unsqueeze(1).broadcast_to([2 * H, B, 2 * KC])).then_inc(sel_in, 16)
            nc.gpsimd.memset(mhl[:, :, 0:96], 0.0).then_inc(mzero, 1)
            rstd_of(0, 1)
            place_keys(2, slice(0, 1), kfirst)
            nc.gpsimd.memset(bqb[:], 0.0).then_inc(consts, 1)
            place_keys(0, slice(1, B), krest)
            rstd_of(0, 2)
            place_keys(1, slice(1, B), krest)
            rstd_of(0, 3)
            pool.wait_ge(late_in, 16)
            for b in range(B):
                last = nc.gpsimd.tensor_copy(vx[:, b].rearrange("p c (h e) -> p (c h) e", e=HD + 1)[:, :, HD],
                                             L["vmask"])
            last.then_inc(vones, 1)
            pool.wait_ge(consts, 2)
            nc.gpsimd.tensor_scalar(bqb[:], bqb[:], L["bq1"], None, ALU.add).then_inc(bq_done, 1)
            for b in range(B):
                add_bias(0, b)
            pool.wait_ge(ints_in, 16)
            nc.gpsimd.tensor_copy(gu_w[:, 0:384], iw[:, ic["gate"]]).then_inc(i_done, 1)
            nc.gpsimd.tensor_copy(gu_w[:, 384:768], iw[:, ic["up"]]).then_inc(i_done, 1)
            nc.gpsimd.tensor_copy(down_w[:], iw[:, ic["down"]]).then_inc(i_done, 1)
            for l, b in norm_order()[B:]:
                rstd_of(l, b)
                if l == 1:
                    add_bias(1, b)

        @block.vector
        def _(dve):
            def ln_begin(l, b):
                n = norm_at[l, b]
                if l == 0:
                    dve.wait_ge(x_in[b], 16)
                else:
                    T.wait_taken(dve, ("y", l - 1, b))
                for t in range(TILES):
                    last = nc.vector.bn_stats(stats[:, b, t], xs[:, b, t])
                last.then_inc(ln_stats, 1)
                dve.wait_ge(ln_stats, n + 1)
                for t in range(TILES):
                    last = nc.vector.bn_aggr(mv[:, b, t], stats[:, b, t])
                last.then_inc(ln_mv, 1)

            def q_lo(b):
                dve.wait_ge(hi_done, hi_at["q", b])
                nc.vector.scalar_tensor_tensor(lo[:, b], ER.bank(("q", b))[:], E["bq0"], hi[:, b].bitcast(F32),
                                               ALU.add, ALU.subtract).then_inc(ER.freed_sem(("q", b)), 1)

            def x_lo(l, b):
                dve.wait_ge(hi_done, hi_at["x", l, b])
                nc.vector.tensor_tensor(lo[:, b], T.bank(("xT", l, b))[:], hi[:, b].bitcast(F32),
                                        ALU.subtract).then_inc(T.freed_sem(("xT", l, b)), 1)

            def keys_lo():
                dve.wait_ge(early_in, 16)
                w = B * KV
                for g in range(G):
                    dve.wait_ge(khi_done, g + 1)
                    mid = khi[32:64, g * w:(g + 1) * w]
                    nc.vector.scalar_tensor_tensor(mid, ER.bank(("k0", g))[32:64, 0:w], E["bk0"][32:64, g:g + 1],
                                                   mid.bitcast(F32), ALU.add,
                                                   ALU.subtract).then_inc(ER.freed_sem(("k0", g)), 1)

            def place_keys(g):
                ER.wait_taken(dve, ("k0", g))
                src = khi[:, g * B * KV:g * B * KV + KV]
                for j in range(HG):
                    col = (g % 2) * (GK + P) + j * KP
                    last = nc.vector.tensor_scalar(kst[0:96, 0, g // 2, col:col + KV], src.bitcast(F32),
                                                   E["headmask"][0:96, j:j + 1], None, ALU.mult)
                if g:
                    last.then_inc(kfirst, 1)

            def queries0_lo(g):
                dve.wait_ge(q0hi_done, g + 1)
                low = qst[64:96, 0, g]
                nc.vector.scalar_tensor_tensor(low, ER.bank(("q0", g))[64:96, :], E["bq0x3"][64:96, g:g + 1],
                                               low.bitcast(F32), ALU.add,
                                               ALU.subtract).then_inc(ER.freed_sem(("q0", g)), 1)

            def values0(b, u):
                key = ("v0", b, u)
                if (b, u) == (0, 0):
                    dve.wait_ge(late_in, 16)
                SR.wait_full(dve, key)
                cs = V_CHUNKS[u]
                v = SR.bank(key)[:, 0:P * len(cs)].rearrange("p (c h e) -> p c h e", c=len(cs), e=HD)
                for half_ in range(2):
                    c0 = half_ * HALF + cs[0]
                    vm = L["vmask"].rearrange("p (c h) -> p c h", h=8)[:, c0:c0 + len(cs)]
                    last = nc.vector.tensor_tensor(
                        vx[:, b, c0:c0 + len(cs)].rearrange("p c (h e) -> p c h e", e=HD + 1)[:, :, :, 0:HD],
                        v[:, :, 8 * half_:8 * half_ + 8], vm.unsqueeze(3).broadcast_to([P, len(cs), 8, HD]), ALU.mult)
                last.then_inc(SR.freed_sem(key), 1)

            def abs_sums():
                dve.wait_ge(late_in, 16)
                for i, name in enumerate(("w1", "w2")):
                    nc.vector.tensor_reduce(gsum[:, i:i + 1], L[name], AX.X, ALU.add,
                                            apply_absolute_value=True).then_inc(dprep, 1)

            def ternary():
                SR.wait_full(dve, ("gamma",))
                n = float(512 * 128)
                g = SR.bank(("gamma",))
                nc.vector.tensor_scalar(thr[:, 0:2], g[:, 0:2], 0.5 / n, 0.5 * EPS, ALU.mult, ALU.add)
                nc.vector.tensor_scalar(thr[:, 2:4], g[:, 0:2], -0.5 / n, -0.5 * EPS, ALU.mult,
                                        ALU.add).then_inc(SR.freed_sem(("gamma",)), 1)
                SR.wait_taken(dve, ("gamma",))
                for i, (name, dst) in enumerate((("w1", w1q), ("w2", w2q))):
                    if i:
                        dve.wait_ge(wq_done, 1)
                    nc.vector.tensor_scalar(below[:], L[name], thr[:, 2 + i:3 + i], None, ALU.is_lt).then_inc(dprep, 1)
                    dve.wait_ge(dprep, 3 + i)
                    nc.vector.scalar_tensor_tensor(dst[:], L[name], thr[:, i:i + 1], below[:], ALU.is_gt,
                                                   ALU.subtract).then_inc(wq_done, 1)

            def maxima(b, t, g):
                key = ("s", b, t, g)
                SR.wait_full(dve, key)
                s_ = SR.bank(key)[:, 0:GK].rearrange("p (h k) -> p h k", h=HG)
                nc.vector.tensor_reduce(mx[:, b, t, HG * g:HG * g + HG], s_[:, :, 0:KV], AX.X,
                                        ALU.max).then_inc(SR.freed_sem(key), 1)

            def max_parts(b):
                for u in s_units()[-3:]:
                    SR.wait_taken(dve, ("s", b, *u))
                if b:
                    T.wait_full(dve, ("m", b - 1))
                else:
                    dve.wait_ge(mzero, 1)
                nc.vector.tensor_copy(mhl[:, :, 96:96 + H].bitcast(F32R), mx[:, b]).then_inc(mhi_done, 1)
                dve.wait_ge(mhi_done, b + 1)
                nc.vector.tensor_tensor(mhl[:, :, 96 + H:P], mx[:, b], mhl[:, :, 96:96 + H],
                                        ALU.subtract).then_inc(mhl_done, 1)

            def normalise(b, pair):
                key = ("av", b, pair)
                T.wait_full(dve, key)
                v = T.bank(key)[:, 0:4 * VW].rearrange("p (h e) -> p h e", e=HD + 1)
                nc.vector.reciprocal(rs[:, b, pair], v[:, :, HD]).then_inc(rs_done, 1)
                dve.wait_ge(rs_done, 2 * b + pair + 1)
                if b >= 2:
                    T.wait_full(dve, ("oT", b - 2))
                nc.vector.tensor_tensor(at0[:, b % 2, 2 * pair:2 * pair + 2].rearrange("p t (h e) -> p (t h) e", e=HD),
                                        v[:, :, 0:HD], rs[:, b, pair].unsqueeze(2).broadcast_to([P, 32, HD]),
                                        ALU.mult).then_inc(T.freed_sem(key), 1)

            def residual(l, b):
                key = ("y", l, b)
                T.wait_full(dve, key)
                src = xs
                if l < 2:
                    dve.wait_ge(bias_done, B * l + b + 1)
                    src = xb
                y = T.bank(key)[:].rearrange("p (t d) -> p t d", t=TILES)
                if l == 2:
                    dve.wait_ge(r1_done, b + 1)
                    for t in range(TILES):
                        last = nc.vector.scalar_tensor_tensor(xs[:, b, t], y[:, t], r1[:, b, t:t + 1], xs[:, b, t],
                                                              ALU.mult, ALU.add)
                else:
                    last = nc.vector.tensor_tensor(xs[:, b], y, src[:, b], ALU.add)
                last.then_inc(T.freed_sem(key), 1)

            def relu(b):
                for f in range(1, F0, 2):
                    key = ("h", b, f)
                    SR.wait_full(dve, key)
                    if b >= 2 and f == 1:
                        T.wait_full(dve, ("y", 1, b - 2))
                    nc.vector.tensor_scalar(hT[:, b % 2, f], SR.bank(key)[:], L["b1"][:, f:f + 1], 0.0, ALU.add,
                                            ALU.max).then_inc(SR.freed_sem(key), 1)

            def keys1():
                SR.wait_full(dve, ("k1",))
                nc.vector.tensor_scalar(k1[:], SR.bank(("k1",))[:, 0:B * KV], L["bk1"], None, ALU.add)\
                    .then_inc(SR.freed_sem(("k1",)), 1)

            def copy_keys1(key, dst):
                SR.wait_full(dve, key)
                nc.vector.tensor_copy(dst[:], SR.bank(key)[:, 0:B * KV]).then_inc(SR.freed_sem(key), 1)

            def values1():
                dve.wait_ge(rows_in, 16)
                SR.wait_full(dve, ("v1",))
                nc.vector.tensor_tensor(v1[:], SR.bank(("v1",))[0:KV, :].rearrange("p (b d) -> p b d", b=B),
                                        R["bv1"][0:KV].unsqueeze(1).broadcast_to([KV, B, D]),
                                        ALU.add).then_inc(SR.freed_sem(("v1",)), 1)

            def softmax1(b):
                key = ("sim", b)
                SR.wait_full(dve, key)
                o = SR.bank(key)[:, 0:TILES * KV].rearrange("p (t k) -> p t k", t=TILES)
                nc.vector.tensor_reduce(m1[:, b], o, AX.X, ALU.max).then_inc(sim_max, 1)
                dve.wait_ge(sim_max, b + 1)
                if b >= 2:
                    dve.wait_ge(p1_done, b - 1)
                nc.vector.tensor_tensor(sm[:, b % 2], o, m1[:, b].unsqueeze(2).broadcast_to([P, TILES, KV]),
                                        ALU.subtract).then_inc(SR.freed_sem(key), 1)

            def sums1(b):
                dve.wait_ge(p1_done, b + 1)
                nc.vector.tensor_reduce(s1[:, b], p1[:, b % 2], AX.X, ALU.add).then_inc(s1_done, 1)
                dve.wait_ge(s1_done, b + 1)
                nc.vector.reciprocal(r1[:, b], s1[:, b]).then_inc(r1_done, 1)

            def gated(b):
                for f in range(F1):
                    key = ("up", b, f)
                    SR.wait_full(dve, key)
                    ER.wait_taken(dve, ("gate", b, f))
                    if b >= 2 and f == 0:
                        T.wait_full(dve, ("y", 3, b - 2))
                    nc.vector.scalar_tensor_tensor(hT[:, b % 2, f], SR.bank(key)[:], QSCALE * QSCALE,
                                                   sg[:, (b * F1 + f) % 3], ALU.mult, ALU.mult)\
                        .then_inc(SR.freed_sem(key), 1)

            ln_begin(0, 0)
            ln_begin(0, 1)
            ln_begin(0, 2)
            keys_lo()
            place_keys(0)
            queries0_lo(0)
            place_keys(1)
            for g in range(1, G):
                queries0_lo(g)
            for n, (t, g) in enumerate(s_units()):
                maxima(0, t, g)
                if n == 9:
                    q_lo(1)
            max_parts(0)
            ln_begin(0, 3)
            for b in range(B):
                if b == 3:
                    abs_sums()
                for k, *n in mix(b):
                    if k == "s":
                        maxima(*n)
                    elif k == "v0":
                        values0(*n)
                    elif k == "av" and n[1] % 2 and n[2]:
                        normalise(n[0], n[1] // 2)
                    elif k == "q":
                        q_lo(*n)
                    elif k == "m":
                        max_parts(*n)
                    elif k == "gamma":
                        ternary()
                    elif k == "k1":
                        keys1()
                    elif k == "kq":
                        copy_keys1(("kq",), kq)
                    elif k == "bq":
                        copy_keys1(("bq",), bqk)
                    elif k == "v1":
                        values1()
                    elif k == "y":
                        residual(*n)
                        ln_begin(1, n[1])
            residual(0, 2)
            ln_begin(1, 2)
            normalise(3, 0)
            x_lo(1, 0)
            normalise(3, 1)
            relu(0)
            x_lo(1, 1)
            residual(0, 3)
            ln_begin(1, 3)
            residual(1, 0)
            ln_begin(2, 0)
            x_lo(1, 2)
            relu(1)
            x_lo(1, 3)
            relu(2)
            residual(1, 1)
            ln_begin(2, 1)
            softmax1(0)
            sums1(0)
            relu(3)
            residual(1, 2)
            ln_begin(2, 2)
            residual(1, 3)
            ln_begin(2, 3)
            softmax1(1)
            sums1(1)
            residual(2, 0)
            ln_begin(3, 0)
            softmax1(2)
            residual(2, 1)
            ln_begin(3, 1)
            softmax1(3)
            sums1(2)
            residual(2, 2)
            x_lo(3, 0)
            ln_begin(3, 2)
            x_lo(3, 1)
            gated(0)
            sums1(3)
            residual(2, 3)
            ln_begin(3, 3)
            x_lo(3, 2)
            gated(1)
            residual(3, 0)
            x_lo(3, 3)
            gated(2)
            residual(3, 1)
            gated(3)
            residual(3, 2)
            residual(3, 3)


def kernel(**inputs):
    import concourse.bacc as bacc
    from concourse.bass_utils import run_bass_kernel_spmd

    a = {k: np.asarray(v) for k, v in inputs.items()}

    def pack(widths, parts, dtype=np.float32):
        cols, n = columns(widths)
        out = np.zeros((P, n), dtype)
        for name, c in cols.items():
            v = parts[name]
            out[:v.shape[0], c] = v.reshape(v.shape[0], -1)
        return out

    ctxp = np.zeros((P, B, 3, KP), np.float32)
    ctxp[:, :, :, :KV] = a["ctx_1024"].transpose(2, 0, 1)[:, :, None, :]

    def three_times(v):
        return np.concatenate([np.tile(v[..., 32 * g:32 * g + 32], 3) for g in range(G)], -1)

    wk0, wq0x3 = three_times(a["L0_xattn_Wk"].T), three_times(a["L0_xattn_Wq"].T)
    bk0x3, bq0x3 = (three_times(a[n]).reshape(G, 96).T for n in ("L0_xattn_bk", "L0_xattn_bq"))
    r = np.arange(96)
    headmask = (r[:, None] % 32 // HD == np.arange(HG)).astype(np.float32)
    hk = np.arange(CH * P).reshape(CH, P).T
    key, head = hk % KP, hk // KP
    vmask = ((key < KV)[:, :, None] & (head[:, :, None] == 8 * (np.arange(CH) // HALF)[None, :, None]
                                       + np.arange(8))).astype(np.float32)
    q = np.arange(P)
    kcol = np.tile(np.arange(KP), HG)
    bf16 = mybir.dt.np(BF16)
    masks = np.where((kcol[None] > q[:, None]) & (kcol[None] < KV), NEG, 0).astype(np.float32)
    maskt = np.where((key[:, :, None] > np.arange(78)) & (key < KV)[:, :, None], NEG, 0).astype(np.float32)
    selector = np.zeros((2, H, 2, KC), np.float32)
    for h in range(H):
        g, j = divmod(h, HG)
        col = (g % 2) * (GK + P) + j * KP
        selector[:, h, g // 2, col:col + KV] = -1.0

    arrays = {
        "x": np.ascontiguousarray(a["x"].reshape(B * S, D)),
        "first": pack(FIRST, {"ident": np.eye(P, dtype=np.float32), "wq0x3": wq0x3, "bq0x3": bq0x3,
                              "wq0": a["L0_xattn_Wq"].T, "bq0": a["L0_xattn_bq"][:, None]}),
        "early": pack(EARLY, {"wk0": wk0, "bk0": bk0x3, "headmask": headmask, "ctxp": ctxp}),
        "masks": pack(MASKS, {"ident16": np.eye(P), "masks": masks, "maskt": maskt}, bf16),
        "late": pack(LATE, {"wv0": a["L0_xattn_Wv"].T, "bv0": a["L0_xattn_bv"][:, None],
                            "wo0": a["L0_xattn_Wo"].T, "w1": a["L0_ffn_W1"].T,
                            "w2": a["L0_ffn_W2"].T.reshape(F0, P, D).transpose(1, 0, 2),
                            "b1": a["L0_ffn_b1"].reshape(F0, P).T,
                            "wk1": a["L1_xattn_Wk"], "wq1": a["L1_xattn_Wq"].T, "wv1": a["L1_xattn_Wv"],
                            "bk1": a["L1_xattn_bk"][:, None], "bq1": a["L1_xattn_bq"][:, None],
                            "vmask": vmask}),
        "rows": np.concatenate([a["L0_xattn_bo"], a["L0_ffn_b2"], a["L1_xattn_bv"]]),
        "ints": pack(INTS, {"gate": a["L1_ffn_w_gate"].T, "up": a["L1_ffn_w_up"].T,
                            "down": a["L1_ffn_w_down"].T.reshape(F1, P, D).transpose(1, 0, 2)}, np.int32),
        "selector": selector.reshape(2 * H, 2 * KC),
    }
    nc = bacc.Bacc("TRN2", target_bir_lowering=False, num_devices=1)
    args = [nc.dram_tensor(f"in_{n}", v.shape, mybir.dt.from_np(v.dtype), kind="ExternalInput").ap()
            for n, v in arrays.items()]
    out = nc.dram_tensor("out", (B * S, D), F32, kind="ExternalOutput").ap()
    build(nc, *args, out)
    got = run_bass_kernel_spmd(nc, [{f"in_{n}": v for n, v in arrays.items()}], core_ids=[0])
    return got.results[0]["out"].reshape(B, S, D)
```
